# Optimizing a Trainium2 kernel written in Bass

```python
import numpy as np
import jax
import jax.numpy as jnp

def _softmax(x, axis=-1):
    return jax.nn.softmax(x, axis=axis)

def _gelu(x):
    return jax.nn.gelu(x, approximate=True)

def _silu(x):
    return jax.nn.silu(x)

def _sigmoid(x):
    return jax.nn.sigmoid(x)

def _layernorm(x, axis=-1, eps=1e-05):
    m = jnp.mean(x, axis=axis, keepdims=True)
    v = jnp.var(x, axis=axis, keepdims=True)
    return (x - m) / jnp.sqrt(v + eps)

def _scatter_add(tgt, idx, src, axis=0):
    return tgt.at[idx].add(src)

def _segment_sum(src, seg, n):
    return jax.ops.segment_sum(src, seg, n)
kernel_name = 'mk_adj_preln_d2_adj_r2_046317'

def setup_inputs(seed: int=0):
    np.random.seed(seed)
    _w = jnp.asarray

    def _rec_inputs():
        import jax
        import jax.numpy as jnp
        _gk = jax.random.key(seed)
        x = -0.0002928 + 1 * jax.random.normal(jax.random.fold_in(_gk, 1), (4096, 256), jnp.float32)
        _w = (1.0 + jnp.arange(4096, dtype=jnp.float32)) ** (-0.5)
        _w = _w / _w.mean()
        _pij = jnp.clip(0.000976562 * _w[:, None] * _w[None, :], 0.0, 1.0)
        _a = jax.random.uniform(jax.random.fold_in(_gk, 2), (4096, 4096)) < _pij
        _a = jnp.logical_or(_a, jnp.swapaxes(_a, -1, -2))
        adj = _a
        return (x, adj)
    x, adj = _rec_inputs()

    def _L0_gnn_setup():
        import jax, jax.numpy as jnp
        import numpy as np
        N = 4096
        D_IN = 256
        D_HID = 512
        D_OUT = 256
        N_NEIGHS = 16
        key = jax.random.key(seed)
        k1, k2, k3 = jax.random.split(key, 3)
        x = jax.random.normal(k1, (N, D_IN), dtype=jnp.float32)
        rows = jnp.arange(N)[:, None]
        cols = (rows + 1 + jnp.arange(N_NEIGHS)[None, :]) % N
        fake_edge_mask = jnp.zeros((N, N), dtype=jnp.bool_).at[rows, cols].set(True)
        real_edge_mask = jnp.zeros((N, N), dtype=jnp.bool_)
        W1 = jax.random.normal(k2, (D_IN, D_HID), dtype=jnp.float32) * (1.0 / np.sqrt(D_IN))
        b1 = jnp.zeros((D_HID,), dtype=jnp.float32)
        W2 = jax.random.normal(k3, (D_HID, D_OUT), dtype=jnp.float32) * (1.0 / np.sqrt(D_HID))
        b2 = jnp.zeros((D_OUT,), dtype=jnp.float32)
        return {'x': x, 'real_edge_mask': real_edge_mask, 'fake_edge_mask': fake_edge_mask, 'W1': W1, 'b1': b1, 'W2': W2, 'b2': b2}
    _L0_gnn_all = _L0_gnn_setup()
    _L0_gnn_in = {k: v for k, v in _L0_gnn_all.items() if k in ('W1', 'b1', 'W2', 'b2')}
    del _L0_gnn_all

    def _L1_gnn_setup():
        import jax, jax.numpy as jnp
        import numpy as np
        N = 4096
        D = 256
        NEG = -1e+30
        key = jax.random.key(seed)
        ks = jax.random.split(key, 5)
        neuron_states = jax.random.normal(ks[0], (N, D), dtype=jnp.float32)
        adjacency = jax.random.bernoulli(ks[1], 0.05, (N, N))
        Wq = jax.random.normal(ks[2], (D, D), dtype=jnp.float32) / np.sqrt(D)
        Wk = jax.random.normal(ks[3], (D, D), dtype=jnp.float32) / np.sqrt(D)
        Wv = jax.random.normal(ks[4], (D, D), dtype=jnp.float32) / np.sqrt(D)
        return {'neuron_states': neuron_states, 'adjacency': adjacency, 'Wq': Wq, 'Wk': Wk, 'Wv': Wv}
    _L1_gnn_all = _L1_gnn_setup()
    _L1_gnn_in = {k: v for k, v in _L1_gnn_all.items() if k in ('Wq', 'Wk', 'Wv')}
    del _L1_gnn_all
    return {'x': x, 'adj': adj, 'L0_gnn_W1': _L0_gnn_in['W1'], 'L0_gnn_b1': _L0_gnn_in['b1'], 'L0_gnn_W2': _L0_gnn_in['W2'], 'L0_gnn_b2': _L0_gnn_in['b2'], 'L1_gnn_Wq': _L1_gnn_in['Wq'], 'L1_gnn_Wk': _L1_gnn_in['Wk'], 'L1_gnn_Wv': _L1_gnn_in['Wv']}

def reference(x, adj, L0_gnn_W1, L0_gnn_b1, L0_gnn_W2, L0_gnn_b2, L1_gnn_Wq, L1_gnn_Wk, L1_gnn_Wv):
    import jax
    import jax.numpy as jnp

    def _L0_gnn_ref(x, real_edge_mask, fake_edge_mask, W1, b1, W2, b2):
        import jax, jax.numpy as jnp
        import numpy as np
        N = 4096
        D_IN = 256
        D_HID = 512
        D_OUT = 256
        N_NEIGHS = 16
        _, idx = jax.lax.top_k(fake_edge_mask.astype(jnp.float32), N_NEIGHS)
        niche_feat = x[idx]
        res = jnp.sum(niche_feat, axis=1) / N_NEIGHS
        hidden = x + res
        h = jax.nn.relu(hidden @ W1 + b1)
        out = h @ W2 + b2
        return out

    def _L1_gnn_ref(neuron_states, adjacency, Wq, Wk, Wv):
        import jax, jax.numpy as jnp
        import numpy as np
        N = 4096
        D = 256
        NEG = -1e+30
        q = neuron_states @ Wq.T
        k = neuron_states @ Wk.T
        v = neuron_states @ Wv.T
        mask = adjacency.T
        scores = jnp.where(mask, q @ k.T, NEG)
        attn = jax.nn.softmax(scores, axis=1)
        attn = jnp.where(mask, attn, 0.0)
        return attn @ v
    h = jnp.maximum(_layernorm(x, axis=-1), 0.0)
    x = x + _L0_gnn_ref(h, adj, adj, L0_gnn_W1, L0_gnn_b1, L0_gnn_W2, L0_gnn_b2)
    h = jnp.maximum(_layernorm(x, axis=-1), 0.0)
    x = x + _L1_gnn_ref(h, adj, L1_gnn_Wq, L1_gnn_Wk, L1_gnn_Wv)
    return x

_drawn_inputs = setup_inputs


def setup_inputs(seed=0):
    import zlib

    import numpy as np

    out = dict(_drawn_inputs(seed))
    spreads = {'L0_gnn_b1': (0.0, 0.1), 'L0_gnn_b2': (0.0, 0.1)}
    factors = {}
    for name, (base, spread) in spreads.items():
        noise = np.random.default_rng([zlib.crc32(name.encode()), seed]).standard_normal(out[name].shape)
        drawn = base * np.exp(spread * noise) if base else spread * noise
        out[name] = jnp.asarray(drawn.astype(out[name].dtype))
    for name, factor in factors.items():
        out[name] = (out[name] * factor).astype(out[name].dtype)
    return out
```

```python
from contextlib import ExitStack, contextmanager

import concourse.bass as bass
from concourse import mybir

ALU = mybir.AluOpType
ACT = mybir.ActivationFunctionType
AX = mybir.AxisListType
F32 = mybir.dt.float32
F16 = mybir.dt.float16
BF16 = mybir.dt.bfloat16
F8 = mybir.dt.float8e4
U8 = mybir.dt.uint8
U16 = mybir.dt.uint16
U32 = mybir.dt.uint32

P = 128
N = 4096
D = 256
HID = 512
F8_ONE = 56.0
PICK = 16
BLK = 512
NB = N // BLK
E = BLK // P
WORDS = N // 4
PAIRS = N // 2
DC = D // P
HC = HID // P
EPS = 1e-5
NEG = -1e30
FLOOR = -1e29
STEPS = 2 * NB
LAG = STEPS + 2
NP = 4
NMASK = 4


class Order:

    def __init__(self, eng, sem):
        self.eng, self.sem, self.base, self.k = eng, sem, 0, 0

    def mark(self, ins):
        ins.then_inc(self.sem, 1)
        self.k += 1

    def wait(self):
        self.eng.wait_ge(self.sem, self.base + self.k)

    @contextmanager
    def loop(self, i, first, last, per):
        outer = self.base + self.k
        self.base, self.k = outer + (i - first) * per, 0
        yield
        assert self.k == per, (self.k, per)
        self.base, self.k = outer + (last - first) * per, 0


def two_layers(nc, x, adj, W1, b1, W2, b2, WqT, WkT, WvT, out):
    x_v = x.rearrange("(b p e) d -> b p e d", b=NB, e=E)
    out_v = out.rearrange("(b p e) d -> b p e d", b=NB, e=E)
    adj_v = adj.rearrange("(b p e) j -> b p e j", b=NB, e=E)
    x1_dram = nc.dram_tensor("x1_scratch", (NB, P, E, D), F32, kind="Internal").ap()
    q_dram = nc.dram_tensor("q_scratch", (NB, P, 2 * DC * BLK), F16, kind="Internal").ap()

    with ExitStack() as ctx:
        def sb(name, shape, dt):
            return ctx.enter_context(nc.sbuf_tensor(name, shape, dt))

        def sem(name):
            return ctx.enter_context(nc.semaphore(name))

        kT = [sb(f"kT_{s}", [P, DC, N], F16) for s in ("hi", "lo")]
        v_hi = sb("v_hi", [P, NB * E, D + 2], F16)
        v_lo = sb("v_lo", [P, NB * E, D], F16)
        ident = sb("ident", [P, P], F32)
        ident16 = sb("ident16", [P, P], F16)
        neg_ident = sb("neg_ident", [P, P], BF16)
        ones = sb("ones", [P, P], F32)
        eps_col = sb("eps_col", [P, 1], F32)

        region = sb("region", [P, 136 * 1024], U8)
        at = [0]

        def carve(shape, dt, size):
            n = size
            for s in shape:
                n *= s
            v = region[:, at[0]:at[0] + n].bitcast(dt)
            at[0] += n
            assert at[0] <= 136 * 1024, at[0]
            names = "abcd"[:len(shape)]
            if len(shape) > 1:
                v = v.rearrange("p (" + " ".join(names) + ") -> p " + " ".join(names),
                                **{m: s for m, s in zip(names, shape)})
            return v

        h_hi = carve([NB * E, D], F16, 2)
        h_lo = carve([NB * E, D], F16, 2)
        picked = carve([2, NB, BLK], U32, 4)
        picked8 = picked.bitcast(F8).rearrange("p a b (i e) -> p a b i e", e=4)
        picked16 = picked.bitcast(U16)
        rows = carve([E, N], U8, 1)
        count = carve([PAIRS + 2], F16, 2)
        w1 = [carve([DC, HID], F16, 2) for _ in range(2)]
        w2 = [carve([HC, D], F16, 2) for _ in range(2)]
        wq = [carve([DC, D], F16, 2) for _ in range(2)]
        wk = [carve([DC, D], F16, 2) for _ in range(2)]
        wv = [carve([DC, D], F16, 2) for _ in range(2)]
        hid_at = at[0]
        hid = [carve([DC, BLK], F16, 2) for _ in range(2)]
        act_f = carve([2, BLK], F32, 4)
        act_h = [carve([HC, BLK], F16, 2) for _ in range(2)]
        x1 = carve([E, D], F32, 4)
        h2 = carve([E, D], F32, 4)
        h2T = [carve([DC, BLK], F16, 2) for _ in range(2)]
        q_out = carve([2, DC, BLK], F16, 2)
        b1_col = carve([HC], F32, 4)
        b2_row = carve([D], F32, 4)
        b2_four = b2_row.unsqueeze(1).to_broadcast([P, E, D])
        falses = carve([PICK], F32, 4)
        false_n = carve([PICK], F32, 4)
        pad = carve([PICK], F32, 4)
        zeros = carve([PICK], F32, 4)
        need = carve([4], F32, 4)[:, 0:1]
        st6 = carve([3, E, 6], F32, 4)
        mean2 = carve([3, E], F32, 4)
        both = carve([3, E], F32, 4)
        apart = carve([3, E], F32, 4)
        var = carve([3, E], F32, 4)
        std = carve([3, E], F32, 4)
        rstd = carve([3, E], F32, 4)
        nbias = carve([3, E], F32, 4)
        x_in = [x1, h2]
        h_f = [act_f.rearrange("p a b -> p (a b)").rearrange("p (e d) -> p e d", e=E),
               region[:, hid_at:hid_at + 4096].bitcast(F32).rearrange("p (e d) -> p e d", e=E)]
        w_f = [act_h[0].rearrange("p a b -> p (a b)").bitcast(F32), act_h[1].rearrange("p a b -> p (a b)").bitcast(F32)]
        at[0] = 0
        ring = carve([STEPS, 2, BLK], F32, 4)
        ring_tile = ring.rearrange("p g u i -> p (g u) i")
        p_hi = carve([NP, 2, BLK], F16, 2)
        p_lo = carve([NP, 2, BLK], F16, 2)
        p_f = carve([2, 2, BLK], F32, 4)
        run_max = carve([2, BLK], F32, 4)
        col_max = carve([BLK], F32, 4)
        diag_max = carve([E, P], F32, 4)
        q_in = carve([2, 2, DC, BLK], F16, 2)
        adj_in = carve([NMASK, E, P], U32, 4)
        mask = carve([2, E, P], U32, 4)
        mask8 = mask.bitcast(F8).rearrange("p m t (i e) -> p m t e i", e=4)
        x1_in = carve([E, D], F32, 4)
        out_sb = carve([E, D], F32, 4)
        max_col = carve([E], F32, 4)
        den = carve([E], F32, 4)
        rden = carve([E], F32, 4)

        ps = ctx.enter_context(nc.psum_tensor("ps", [P, 8, BLK], F32))
        agg = ps[:, 0:2, :]
        tp = ps[:, 2:4, :]
        tp16 = tp.bitcast(U16)
        pa = ps[:, 4:8, :]
        sc = ps[:, 0:2, :]
        mc = ps[:, 3, :]
        acc = ps[:, 4:8, :]

        adj_loaded = [sem(f"adj_loaded{q}") for q in range(E)]
        x_loaded = [sem(f"x_loaded{i}") for i in range(2)]
        w_loaded = [sem(f"w_loaded{i}") for i in range(2)]
        b_loaded, xres_loaded, x1_stored, q_stored = sem("b_loaded"), sem("xres_loaded"), sem("x1_stored"), sem("q_stored")
        mask_loaded, q_loaded, x1_loaded, out_stored = sem("mask_loaded"), sem("q_loaded"), sem("x1_loaded"), sem("out_stored")
        consts_ready, w_split, pool_order, dve_order = sem("consts_ready"), sem("w_split"), sem("pool_order"), sem("dve_order")
        dve_consts = sem("dve_consts")
        ln0_stats, ln0_std, ln0_scale, ln0_h, h_hi_ready, h_ready = (sem(s) for s in (
            "ln0_stats", "ln0_std", "ln0_scale", "ln0_h", "h_hi_ready", "h_ready"))
        picks_ready, tp_ready, picks_stored = sem("picks_ready"), sem("tp_ready"), sem("picks_stored")
        agg_done, hid_hi, hid_lo = sem("agg_done"), sem("hid_hi"), sem("hid_lo")
        up_done, act_ready, act_lo = sem("up_done"), sem("act_ready"), sem("act_lo")
        down_done, xres_ready, x1_ready = sem("down_done"), sem("xres_ready"), sem("x1_ready")
        ln1_stats, ln1_std, ln1_scale, h2_ready = sem("ln1_stats"), sem("ln1_std"), sem("ln1_scale"), sem("h2_ready")
        h2T_done, h2T_hi, h2T_lo = sem("h2T_done"), sem("h2T_hi"), sem("h2T_lo")
        q_done, q_hi, q_lo = sem("q_done"), sem("q_hi"), sem("q_lo")
        k_done, k_hi, k_lo = sem("k_done"), sem("k_hi"), sem("k_lo")
        v_done, v_hi_s, v_lo_s = sem("v_done"), sem("v_hi_s"), sem("v_lo_s")
        qk_done, copied, maxed, colmax_ready, maxT_done = (sem(s) for s in (
            "qk_done", "copied", "maxed", "colmax_ready", "maxT_done"))
        diag_ready, max_spread, shifted, exp_done, p_ready = (sem(s) for s in (
            "diag_ready", "max_spread", "shifted", "exp_done", "p_ready"))
        mask_ready, pv_done, out_ready = sem("mask_ready"), sem("pv_done"), sem("out_ready")

        block = ctx.enter_context(nc.Block())


        @block.sync
        def _(sp):

            def load_rows(b, q):
                sp.dma_start(rows[:, q, :], adj_v[b, :, q, :]).then_inc(adj_loaded[q], 16)

            def load_x(c):
                if c >= 2:
                    sp.wait_ge(ln0_h, c - 1)
                sp.dma_start(x_in[c % 2], x_v[c]).then_inc(x_loaded[c % 2], 16)

            load_rows(0, 0)
            load_x(0)
            load_x(1)
            load_rows(0, 1)
            load_rows(0, 2)
            load_rows(0, 3)
            sp.dma_start(b1_col, b1.rearrange("(c p) -> p c", p=P),
                         allow_slow_non_contiguous=True).then_inc(b_loaded, 16)
            sp.dma_start(b2_row, b2.unsqueeze(0).to_broadcast([P, D])).then_inc(b_loaded, 16)
            for c in range(2, NB):
                load_x(c)
            def post_traffic(b):
                sp.wait_ge(x1_ready, b + 1)
                sp.dma_start(x1_dram[b], x1).then_inc(x1_stored, 16)
                sp.wait_ge(q_lo, b + 1)
                sp.dma_start(q_dram[b], q_out.rearrange("p s c i -> p (s c i)")).then_inc(q_stored, 16)
                sp.wait_ge(x1_stored, 16 * (b + 1))
                sp.wait_ge(q_stored, 16 * (b + 1))
                if b is not NB - 1:
                    sp.dma_start(x1, x_v[b + 1]).then_inc(xres_loaded, 16)

            sp.wait_ge(ln0_h, NB)
            sp.dma_start(x1, x_v[0]).then_inc(xres_loaded, 16)
            with sp.Fori(0, NB - 1) as b:
                post_traffic(b)
            post_traffic(NB - 1)

            def load_q(i):
                if i is 0:
                    sp.wait_ge(q_stored, 16 * NB)
                if i is 1:
                    sp.wait_ge(q_loaded, 16)
                sp.dma_start(q_in[:, i % 2].rearrange("p s c i -> p (s c i)"), q_dram[i]).then_inc(q_loaded, 16)

            def load_x1(i):
                if i is 0:
                    sp.wait_ge(x1_stored, 16 * NB)
                else:
                    sp.wait_ge(out_stored, 16 * i)
                sp.dma_start(x1_in, x1_dram[i]).then_inc(x1_loaded, 16)

            def store_out(i):
                sp.wait_ge(out_ready, i + 1)
                sp.dma_start(out_v[i], out_sb).then_inc(out_stored, 16)

            sp.wait_ge(v_lo_s, NB + 1)
            load_q(0)
            load_q(1)
            load_x1(0)
            with sp.Fori(2, NB) as i:
                sp.wait_ge(q_loaded, 16 * i)
                sp.wait_ge(qk_done, E * NB * (i - 1))
                load_q(i)
                store_out(i - 2)
                load_x1(i - 1)
            store_out(NB - 2)
            load_x1(NB - 1)
            store_out(NB - 1)
            sp.wait_ge(out_stored, 16 * NB)
            sp.wait_ge(x1_stored, 16 * NB)
            sp.wait_ge(q_stored, 16 * NB)

        @block.gpsimd
        def _(pool):
            order = Order(pool, pool_order)
            order.mark(nc.gpsimd.memset(ident[:], 0.0))
            order.mark(nc.gpsimd.memset(ident16[:], 0.0))
            order.mark(nc.gpsimd.memset(neg_ident[:], 0.0))
            order.wait()
            for t, val in ((ident, 1.0), (ident16, float(PICK)), (neg_ident, NEG / 2)):
                nc.gpsimd.affine_select(out=t[:], in_=t[:], compare_op=ALU.not_equal, fill=val, base=0,
                                        pattern=[[-1, P]], channel_multiplier=1).then_inc(consts_ready, 1)
            nc.gpsimd.memset(ones[:], 1.0).then_inc(consts_ready, 1)
            nc.gpsimd.memset(v_hi[:, :, D:D + 1], 1.0).then_inc(consts_ready, 1)

            loads = ((W1.rearrange("(c p) n -> p c n", p=P), w1), (W2.rearrange("(c p) n -> p c n", p=P), w2),
                     (WqT.rearrange("(c p) n -> p c n", p=P), wq), (WkT.rearrange("(c p) n -> p c n", p=P), wk),
                     (WvT.rearrange("(c p) n -> p c n", p=P), wv))

            def load_w(n):
                src, w = loads[n]
                c = src.shape[1]
                dst = w_f[n % 2][:, 0:c * src.shape[2]].rearrange("p (c n) -> p c n", c=c)
                pool.dma_start(dst, src).then_inc(w_loaded[n % 2], 16)
                return dst

            def split_w(n, src):
                w = loads[n][1]
                pool.wait_ge(w_loaded[n % 2], 16 * (n // 2 + 1))
                order.mark(nc.gpsimd.tensor_copy(w[0], src))
                order.wait()
                nc.gpsimd.tensor_tensor(w[1], src, w[0], ALU.subtract).then_inc(w_split, 1)

            def split_h(c):
                pool.wait_ge(h_hi_ready, c + 1)
                nc.gpsimd.tensor_tensor(h_lo[:, c * E:(c + 1) * E, :], h_f[c % 2],
                                        h_hi[:, c * E:(c + 1) * E, :], ALU.subtract).then_inc(h_ready, 1)

            held = [load_w(0), load_w(1)]
            for c in range(NB):
                split_h(c)
            for n in range(len(loads)):
                split_w(n, held[n])
                if n + 2 < len(loads):
                    pool.wait_ge(w_split, n + 1)
                    held.append(load_w(n + 2))

            def post(b):
                pool.wait_ge(xres_loaded, 16 * (b + 1))
                nc.gpsimd.tensor_tensor(x1, x1, b2_four, ALU.add).then_inc(xres_ready, 1)
                for c in range(HC):
                    pool.wait_ge(act_ready, HC * b + c + 1)
                    nc.gpsimd.tensor_tensor(act_h[1][:, c, :], act_f[:, c % 2, :], act_h[0][:, c, :],
                                            ALU.subtract).then_inc(act_lo, 1)

            pool.wait_ge(b_loaded, 32)
            with pool.Fori(0, NB) as b:
                post(b)

        @block.vector
        def _(dve):
            order = Order(dve, dve_order)
            nc.vector.memset(eps_col[:], EPS).then_inc(dve_consts, 1)
            nc.vector.memset(need, 0.0).then_inc(v_lo_s, 1)
            order.mark(nc.vector.memset(zeros, 0.0))
            order.mark(nc.vector.memset(count[:, 0:1], 0.0))
            order.wait()

            def pieces(b, q):
                byte = rows[:, q, :].rearrange("p (w t) -> p w t", t=2)
                pick = rows[:, q, :].bitcast(F8).rearrange("p (w t) -> p w t", t=2)
                first16 = rows[:, q, 0:PICK]
                half = PAIRS // 2

                def count_first():
                    dve.wait_ge(adj_loaded[q], 16 * (b + 1))
                    order.mark(nc.vector.tensor_tensor_scan(count[:, 1:half + 1], byte[:, 0:half, 0],
                                                            byte[:, 0:half, 1], 0.0, ALU.add, ALU.add))
                    order.mark(nc.vector.tensor_scalar(falses, first16, -F8_ONE, F8_ONE, ALU.mult, ALU.add))

                def count_second():
                    order.wait()
                    order.mark(nc.vector.tensor_tensor_scan(count[:, half + 1:PAIRS + 1], byte[:, half:, 0],
                                                            byte[:, half:, 1], count[:, half:half + 1],
                                                            ALU.add, ALU.add))
                    order.mark(nc.vector.tensor_tensor_scan(false_n, falses, zeros, 0.0, ALU.add, ALU.add))
                    order.wait()

                def pick_odd():
                    order.mark(nc.vector.tensor_scalar(need, count[:, PAIRS:PAIRS + 1], -F8_ONE,
                                                       PICK * F8_ONE, ALU.mult, ALU.add))
                    order.mark(nc.vector.scalar_tensor_tensor(pick[:, :, 1], count[:, 1:PAIRS + 1], float(PICK),
                                                              byte[:, :, 1], ALU.is_le, ALU.mult, saturate=False))
                    order.wait()

                def pick_even():
                    order.mark(nc.vector.scalar_tensor_tensor(pad, false_n, need, falses, ALU.is_le, ALU.mult))
                    order.mark(nc.vector.scalar_tensor_tensor(pick[:, :, 0], count[:, 0:PAIRS], float(PICK - 1),
                                                              byte[:, :, 0], ALU.is_le, ALU.mult, saturate=False))
                    order.wait()
                    nc.vector.tensor_tensor(first16, first16, pad, ALU.add).then_inc(picks_ready, 1)

                return [count_first, count_second, pick_odd, pick_even]

            def stats(src, s):
                for e in range(E):
                    last = nc.vector.bn_stats(st6[:, s, e, :], src[:, e, :])
                order.mark(last)
                order.wait()
                even, odd = st6[:, s, :, 0:3], st6[:, s, :, 3:6]
                nc.vector.tensor_tensor(mean2[:, s, :], even[:, :, 1], odd[:, :, 1], ALU.add)
                nc.vector.tensor_tensor(both[:, s, :], even[:, :, 2], odd[:, :, 2], ALU.add)
                order.mark(nc.vector.tensor_tensor(apart[:, s, :], even[:, :, 1], odd[:, :, 1], ALU.subtract))
                order.wait()
                order.mark(nc.vector.tensor_tensor(apart[:, s, :], apart[:, s, :], apart[:, s, :], ALU.mult))
                order.wait()
                return nc.vector.scalar_tensor_tensor(var[:, s, :], apart[:, s, :], D / 4.0, both[:, s, :],
                                                      ALU.mult, ALU.add)

            def scale(s):
                order.mark(nc.vector.reciprocal(rstd[:, s, :], std[:, s, :]))
                order.wait()
                return nc.vector.scalar_tensor_tensor(nbias[:, s, :], mean2[:, s, :], -0.5, rstd[:, s, :],
                                                      ALU.mult, ALU.mult)

            def ln0_a(c):
                dve.wait_ge(x_loaded[c % 2], 16 * (c // 2 + 1))
                if c >= 2:
                    dve.wait_ge(ln0_h, c - 1)
                stats(x_in[c % 2], c % 2).then_inc(ln0_stats, 1)

            def ln0_b(c):
                dve.wait_ge(ln0_std, c + 1)
                scale(c % 2).then_inc(ln0_scale, 1)

            for j in range(4):
                ln0_a(2 * j)
                ln0_a(2 * j + 1)
                for n, piece in enumerate(pieces(0, j)):
                    piece()
                    if n < 2:
                        ln0_b(2 * j + n)
            for q in range(2):
                for piece in pieces(1, q):
                    piece()

            def hid_low(b):
                dve.wait_ge(hid_hi, b + 1)
                nc.vector.scalar_tensor_tensor(hid[1], agg, 1.0 / PICK, hid[0], ALU.mult,
                                               ALU.subtract).then_inc(hid_lo, 1)

            def iteration(b, rows_ahead, post, agg_too=True):
                todo = []
                if rows_ahead >= 2:
                    todo += pieces(b + 1, 2) + pieces(b + 1, 3)
                if rows_ahead >= 4:
                    todo += pieces(b + 2, 0) + pieces(b + 2, 1)
                pb = b - 1

                def run(n):
                    for _ in range(min(n, len(todo))):
                        todo.pop(0)()

                run(10)
                if post:
                    dve.wait_ge(down_done, pb + 1)
                    dve.wait_ge(xres_ready, pb + 1)
                    nc.vector.tensor_tensor(x1, pa[:, 0:2, :].rearrange("p a (t d) -> p (a t) d", d=D), x1,
                                            ALU.add).then_inc(x1_ready, 1)
                    dve.wait_ge(x1_ready, pb + 1)
                    stats(x1, 2).then_inc(ln1_stats, 1)
                run(1)
                if post:
                    dve.wait_ge(ln1_std, pb + 1)
                    scale(2).then_inc(ln1_scale, 1)
                run(2)
                if post:
                    dve.wait_ge(h2T_hi, pb + 1)
                    nc.vector.tensor_tensor(h2T[1], pa[:, 2:4, :], h2T[0], ALU.subtract).then_inc(h2T_lo, 1)
                run(2)
                if post:
                    dve.wait_ge(q_hi, pb + 1)
                    nc.vector.tensor_tensor(q_out[:, 1], pa[:, 0:2, :], q_out[:, 0], ALU.subtract).then_inc(q_lo, 1)
                run(9)
                if agg_too:
                    hid_low(b)
                if post:
                    dve.wait_ge(k_hi, pb + 1)
                    nc.vector.tensor_tensor(kT[1][:, :, bass.ts(pb, BLK)], pa[:, 2:4, :],
                                            kT[0][:, :, bass.ts(pb, BLK)], ALU.subtract).then_inc(k_lo, 1)
                    dve.wait_ge(v_hi_s, pb + 1)
                    nc.vector.tensor_tensor(v_lo[:, bass.ts(pb, E), :],
                                            pa[:, 0:2, :].rearrange("p a (t d) -> p (a t) d", d=D),
                                            v_hi[:, bass.ts(pb, E), 0:D], ALU.subtract).then_inc(v_lo_s, 1)

            iteration(0, 4, False)
            with dve.Fori(1, NB - 2) as b, order.loop(b, 1, NB - 2, 4 * 8 + 4):
                iteration(b, 4, True)
            iteration(NB - 2, 2, True)
            iteration(NB - 1, 0, True)
            iteration(NB, 0, True, agg_too=False)

            def flip_mask(i, jb, par):
                n = i * NB + jb
                dve.wait_ge(mask_loaded, 16 * (n + 1))
                if not (i is 0 and jb is par):
                    dve.wait_ge(qk_done, E * (n - 1))
                nc.vector.tensor_scalar(mask[:, par], adj_in[:, jb % NMASK], 0x01010101, 6, ALU.bitwise_xor,
                                        ALU.logical_shift_left).then_inc(mask_ready, 1)

            def running_max(i, g):
                dve.wait_ge(copied, 2 * (i * STEPS + g) + 2)
                if g is 1:
                    nc.vector.tensor_tensor(run_max, ring[:, 0], ring[:, 1], ALU.max).then_inc(maxed, 1)
                else:
                    dve.wait_ge(maxed, i * (STEPS - 1) + g - 1)
                    nc.vector.tensor_tensor(run_max, run_max, ring[:, g], ALU.max).then_inc(maxed, 1)

            def column_max(i):
                dve.wait_ge(maxed, (i + 1) * (STEPS - 1))
                nc.vector.tensor_tensor(col_max, run_max[:, 0], run_max[:, 1], ALU.max).then_inc(colmax_ready, 1)
                dve.wait_ge(maxT_done, i + 1)
                order.mark(nc.vector.tensor_reduce(max_col, mc.rearrange("p (e q) -> p e q", e=E), axis=AX.X,
                                                   op=ALU.max))
                order.wait()
                order.mark(nc.vector.tensor_scalar(max_col, max_col, FLOOR, None, ALU.max))
                order.wait()
                nc.vector.tensor_tensor(diag_max, ident[:].unsqueeze(1).to_broadcast([P, E, P]),
                                        max_col.unsqueeze(2).to_broadcast([P, E, P]),
                                        ALU.mult).then_inc(diag_ready, 1)
                dve.wait_ge(max_spread, i + 1)

            def shift(m, g):
                nc.vector.tensor_tensor(ring[:, g], ring[:, g], mc.unsqueeze(1).to_broadcast([P, 2, BLK]),
                                        ALU.subtract).then_inc(shifted, 1)

            def prob_low(m, slot):
                dve.wait_ge(exp_done, m + 1)
                nc.vector.tensor_tensor(p_lo[:, slot], p_f[:, slot % 2], p_hi[:, slot],
                                        ALU.subtract).then_inc(p_ready, 1)

            def finish(i):
                dve.wait_ge(pv_done, (i + 1) * STEPS)
                order.mark(nc.vector.tensor_scalar(den, acc[:, :, D], 1e-30, None, ALU.max))
                order.wait()
                order.mark(nc.vector.reciprocal(rden, den))
                dve.wait_ge(x1_loaded, 16 * (i + 1))
                order.wait()
                for e in range(E):
                    last = nc.vector.scalar_tensor_tensor(out_sb[:, e, :], acc[:, e, 0:D], rden[:, e:e + 1],
                                                          x1_in[:, e, :], ALU.mult, ALU.add)
                last.then_inc(out_ready, 1)

            def step(i, g, r, scores=True, probs=True):
                n = i * STEPS + g
                if probs:
                    shift(n - STEPS + 1, g + 1)
                if scores and g is not 0:
                    running_max(i, g)
                if probs:
                    prob_low(n - STEPS + 1, (r + 1) % NP)

            def query_block(i, scores, probs, finishes):
                step(i, 0, 0, scores, probs)
                if scores:
                    flip_mask(i, 1, 1)
                step(i, 1, 1, scores, probs)
                if finishes:
                    finish(i - 2)
                step(i, 2, 2, scores, probs)
                if scores:
                    flip_mask(i, 2, 0)
                step(i, 3, 3, scores, probs)
                with dve.Fori(1, 3) as k:
                    for r in range(4):
                        step(i, 4 * k + r, r, scores, probs)
                        if scores and r % 2 == 0:
                            flip_mask(i, 2 * k + 1 + r // 2, 1 - r // 2)
                for r in range(3):
                    step(i, 12 + r, r, scores, probs)
                    if scores and r == 0:
                        flip_mask(i, 7, 1)

            def boundary(i, more):
                if more:
                    flip_mask(i + 1, 0, 0)
                running_max(i, STEPS - 1)
                column_max(i)
                shift(i * STEPS, 0)
                prob_low(i * STEPS, 0)

            dve.wait_ge(x1_stored, 16 * NB)
            dve.wait_ge(q_stored, 16 * NB)
            flip_mask(0, 0, 0)
            query_block(0, True, False, False)
            boundary(0, True)
            query_block(1, True, True, False)
            boundary(1, True)
            with dve.Fori(2, NB - 1) as i, order.loop(i, 2, NB - 1, 4):
                query_block(i, True, True, True)
                boundary(i, True)
            query_block(NB - 1, True, True, True)
            boundary(NB - 1, False)
            query_block(NB, False, True, True)
            finish(NB - 1)

        @block.scalar
        def _(act):
            act.wait_ge(dve_consts, 1)

            def ln0(c):
                act.wait_ge(ln0_stats, c + 1)
                nc.scalar.activation(std[:, c % 2, :], var[:, c % 2, :], ACT.Sqrt, scale=1.0 / D,
                                     bias=eps_col[:]).then_inc(ln0_std, 1)
                act.wait_ge(ln0_scale, c + 1)
                if c >= 2:
                    act.wait_ge(h_ready, c - 1)
                for e in range(E):
                    last = nc.scalar.activation(h_f[c % 2][:, e, :], x_in[c % 2][:, e, :], ACT.Relu,
                                                scale=rstd[:, c % 2, e:e + 1], bias=nbias[:, c % 2, e:e + 1])
                last.then_inc(ln0_h, 1)
                act.wait_ge(ln0_h, c + 1)
                nc.scalar.copy(h_hi[:, c * E:(c + 1) * E, :], h_f[c % 2]).then_inc(h_hi_ready, 1)

            def store_picks(b, q, h):
                act.wait_ge(tp_ready, 8 * b + 2 * q + h + 1)
                nc.scalar.copy(picked16[:, b % 2, 4 * h:4 * h + 4, 2 * P * q:2 * P * (q + 1)],
                               tp16[:, h, :].rearrange("p (c i) -> p c i", c=4)).then_inc(picks_stored, 1)

            def hid_high(b):
                act.wait_ge(agg_done, b + 1)
                nc.scalar.activation(hid[0], agg, ACT.Copy, scale=1.0 / PICK).then_inc(hid_hi, 1)

            def relu(b, c):
                act.wait_ge(up_done, HC * b + c + 1)
                if c >= 2:
                    act.wait_ge(act_lo, HC * b + c - 1)
                nc.scalar.activation(act_f[:, c % 2, :], pa[:, c, :], ACT.Relu, bias=b1_col[:, c:c + 1])
                nc.scalar.activation(act_h[0][:, c, :], pa[:, c, :], ACT.Relu,
                                     bias=b1_col[:, c:c + 1]).then_inc(act_ready, 1)

            def post_ops(b):
                def ups(c):
                    return lambda: (relu(b, c), relu(b, c + 1))

                def std_():
                    act.wait_ge(ln1_stats, b + 1)
                    nc.scalar.activation(std[:, 2, :], var[:, 2, :], ACT.Sqrt, scale=1.0 / D,
                                         bias=eps_col[:]).then_inc(ln1_std, 1)

                def norm():
                    act.wait_ge(ln1_scale, b + 1)
                    for e in range(E):
                        last = nc.scalar.activation(h2[:, e, :], x1[:, e, :], ACT.Relu,
                                                    scale=rstd[:, 2, e:e + 1], bias=nbias[:, 2, e:e + 1])
                    last.then_inc(h2_ready, 1)

                def turn():
                    act.wait_ge(h2T_done, b + 1)
                    nc.scalar.copy(h2T[0], pa[:, 2:4, :]).then_inc(h2T_hi, 1)

                def q_():
                    act.wait_ge(q_done, b + 1)
                    if b is not 0:
                        act.wait_ge(q_stored, 16 * b)
                    nc.scalar.copy(q_out[:, 0], pa[:, 0:2, :]).then_inc(q_hi, 1)

                def kv():
                    act.wait_ge(k_done, b + 1)
                    nc.scalar.copy(kT[0][:, :, bass.ts(b, BLK)], pa[:, 2:4, :]).then_inc(k_hi, 1)
                    act.wait_ge(v_done, b + 1)
                    nc.scalar.copy(v_hi[:, bass.ts(b, E), 0:D],
                                   pa[:, 0:2, :].rearrange("p a (t d) -> p (a t) d", d=D)).then_inc(v_hi_s, 1)

                return {0: ups(0), 1: ups(2), 4: std_, 5: norm, 6: turn, 7: q_, 8: kv}

            def load_rows(b, q):
                act.dma_start(rows[:, q, :], adj_v[b, :, q, :]).then_inc(adj_loaded[q], 16)

            for c in range(NB):
                ln0(c)
                if c % 2:
                    store_picks(0, c // 2, 0)
                    store_picks(0, c // 2, 1)
                    load_rows(1, c // 2)
            act.wait_ge(b_loaded, 32)

            def iteration(b, turn, load, post, agg_too=True):
                ops = post_ops(b - 1) if post else {}
                for s in range(NB):
                    if turn:
                        store_picks(b + 1, s // 2, s % 2)
                        if load and s % 2:
                            load_rows(b + 2, s // 2)
                    if s in ops:
                        ops[s]()
                if agg_too:
                    hid_high(b)
                if post:
                    ops[NB]()

            iteration(0, True, True, False)
            with act.Fori(1, NB - 2) as b:
                iteration(b, True, True, True)
            iteration(NB - 2, True, False, True)
            iteration(NB - 1, False, False, True)
            iteration(NB, False, False, True, agg_too=False)

            def copy_scores(i, g, r):
                if i is not 0:
                    act.wait_ge(exp_done, i * STEPS + g - STEPS + 1)
                for u in range(2):
                    t = 2 * (i * STEPS + g) + u
                    act.wait_ge(qk_done, t + 1)
                    nc.scalar.copy(ring_tile[:, 2 * g + u, :], sc[:, u, :]).then_inc(copied, 1)

            def probs(m, g, slot, later=True):
                act.wait_ge(shifted, m + 1)
                if later:
                    act.wait_ge(pv_done, m - NP + 1)
                nc.scalar.activation(p_hi[:, slot], ring[:, g], ACT.Exp)
                nc.scalar.activation(p_f[:, slot % 2], ring[:, g], ACT.Exp).then_inc(exp_done, 1)

            def load_mask(i, jb):
                if isinstance(jb, int) and jb >= NB:
                    i, jb = i + 1, jb - NB
                n = i * NB + jb
                early = i is 0 and isinstance(jb, int)
                if not (early and jb == 0):
                    act.wait_ge(mask_loaded, 16 * n)
                if not (early and jb < NMASK):
                    act.wait_ge(mask_ready, n - NMASK + 1)
                act.dma_start(adj_in[:, jb % NMASK].bitcast(U8),
                              adj_v[jb, :, :, bass.ts(i, BLK)]).then_inc(mask_loaded, 16)

            def step(i, g, r, scores=True, prob=True):
                if scores:
                    copy_scores(i, g, r)
                if prob:
                    probs(i * STEPS + g - STEPS + 1, g + 1, (r + 1) % NP)

            def query_block(i, scores, prob, more=True):
                for r in range(4):
                    if i is 1 and r < 3:
                        copy_scores(i, r, r)
                        probs(r + 1, r + 1, (r + 1) % NP, later=False)
                    else:
                        step(i, r, r, scores, prob)
                    if scores and r % 2 == 0:
                        load_mask(i, 2 + r // 2)
                with act.Fori(1, 3) as k:
                    for r in range(4):
                        step(i, 4 * k + r, r, scores, prob)
                        if scores and r % 2 == 0:
                            load_mask(i, 2 * k + 2 + r // 2)
                for r in range(3):
                    step(i, 12 + r, r, scores, prob)
                    if scores and more and r % 2 == 0:
                        load_mask(i, NB + r // 2)

            def boundary(i):
                copy_scores(i, STEPS - 1, 3)
                probs(i * STEPS, 0, 0, later=i is not 0)

            act.wait_ge(x1_stored, 16 * NB)
            act.wait_ge(q_stored, 16 * NB)
            act.wait_ge(v_lo_s, NB + 1)
            load_mask(0, 0)
            load_mask(0, 1)
            query_block(0, True, False)
            boundary(0)
            query_block(1, True, True)
            boundary(1)
            with act.Fori(2, NB - 1) as i:
                query_block(i, True, True)
                boundary(i)
            query_block(NB - 1, True, True, more=False)
            boundary(NB - 1)
            query_block(NB, False, True)

        @block.tensor
        def _(pe):
            rows_w = rows.bitcast(F32)
            terms = ((0, 0), (0, 1), (1, 0))

            def turn_picks(b, q, h, first=False, summed=None):
                pe.wait_ge(picks_ready, E * b + q + 1)
                if not first:
                    pe.wait_ge(picks_stored, 8 * b + 2 * q + h - 1)
                for c in range(4):
                    if summed is not None and c == 3:
                        await_sum(summed)
                    w = (4 * h + c) * P
                    last = nc.tensor.transpose(tp[:, h, c * P:(c + 1) * P], rows_w[:, q, w:w + P], ident[:])
                last.then_inc(tp_ready, 1)

            def await_sum(b):
                if b is not 0:
                    pe.wait_ge(hid_lo, b)
                pe.wait_ge(picks_stored, 8 * (b + 1))

            def sum_picks(b, c, par):
                if b is 0:
                    pe.wait_ge(h_ready, c + 1)
                for e in range(E):
                    for half in (h_hi, h_lo):
                        for d in range(DC):
                            nc.tensor.matmul(agg[:, d, :], half[:, c * E + e, d * P:(d + 1) * P],
                                             picked8[:, par, c, :, e], start=(c == 0 and e == 0 and half is h_hi),
                                             stop=False)
                if c == NB - 1:
                    for e in range(E):
                        for half in (h_hi, h_lo):
                            for d in range(DC):
                                last = nc.tensor.matmul(agg[:, d, e * P:(e + 1) * P],
                                                        half[:, b * E + e, d * P:(d + 1) * P], ident16[:],
                                                        start=False, stop=(e == E - 1 and half is h_lo))
                    last.then_inc(agg_done, 1)

            def up(b, c):
                n = 0
                for s, t in terms:
                    for d in range(DC):
                        last = nc.tensor.matmul(pa[:, c, :], w1[s][:, d, c * P:(c + 1) * P], hid[t][:, d, :],
                                                start=(n == 0), stop=(n == 5))
                        n += 1
                last.then_inc(up_done, 1)

            def down(b):
                pe.wait_ge(act_lo, HC * (b + 1))
                for e in range(E):
                    n = 0
                    for s, t in terms:
                        for c in range(HC):
                            last = nc.tensor.matmul(pa[:, e // 2, (e % 2) * D:(e % 2 + 1) * D],
                                                    act_h[s][:, c, e * P:(e + 1) * P], w2[t][:, c, :],
                                                    start=(n == 0), stop=(n == 11))
                            n += 1
                last.then_inc(down_done, 1)

            def turn_h2(b):
                pe.wait_ge(h2_ready, b + 1)
                for d in range(DC):
                    for e in range(E):
                        last = nc.tensor.transpose(pa[:, 2 + d, e * P:(e + 1) * P], h2[:, e, d * P:(d + 1) * P],
                                                   ident[:])
                last.then_inc(h2T_done, 1)

            def project_T(w, bank, done):
                for d in range(DC):
                    n = 0
                    for s, t in terms:
                        for c in range(DC):
                            last = nc.tensor.matmul(pa[:, bank + d, :], w[s][:, c, d * P:(d + 1) * P],
                                                    h2T[t][:, c, :], start=(n == 0), stop=(n == 5))
                            n += 1
                last.then_inc(done, 1)

            def project_v(b):
                pe.wait_ge(q_lo, b + 1)
                for e in range(E):
                    n = 0
                    for s, t in terms:
                        for c in range(DC):
                            last = nc.tensor.matmul(pa[:, e // 2, (e % 2) * D:(e % 2 + 1) * D],
                                                    h2T[s][:, c, e * P:(e + 1) * P], wv[t][:, c, :],
                                                    start=(n == 0), stop=(n == 5))
                            n += 1
                last.then_inc(v_done, 1)

            def post_stage(b, s):
                if s == 0:
                    pe.wait_ge(hid_lo, b + 1)
                    pe.wait_ge(v_lo_s, b + 1)
                    up(b, 0)
                    up(b, 1)
                if s == 1:
                    up(b, 2)
                    up(b, 3)
                if s == 3:
                    down(b)
                if s == 5:
                    turn_h2(b)
                if s == 6:
                    pe.wait_ge(h2T_lo, b + 1)
                    project_T(wq, 0, q_done)
                if s == 7:
                    project_T(wk, 2, k_done)
                    project_v(b)

            def iteration(b, par, turn, post, agg_too=True):
                for s in range(NB):
                    if turn:
                        turn_picks(b + 1, s // 2, s % 2, summed=b if s == 0 else None)
                    elif agg_too and s == 0:
                        await_sum(b)
                    if agg_too:
                        sum_picks(b, s, par)
                    if post:
                        post_stage(b - 1, s)

            pe.wait_ge(consts_ready, 5)
            for q in range(E):
                for h in range(2):
                    turn_picks(0, q, h, first=q == 0)
            iteration(0, 0, True, False)
            pe.wait_ge(w_split, 5)
            with pe.Fori(0, NB // 2 - 1) as j:
                iteration(2 * j + 1, 1, True, True)
                iteration(2 * j + 2, 0, True, True)
            iteration(NB - 1, 1, False, True)
            iteration(NB, 0, False, True, agg_too=False)

            def scores(i, g, jb, r):
                for u in range(2):
                    tile = 2 * g + u
                    t = i * STEPS * 2 + tile
                    if u == 0 and r % 2 == 0:
                        pe.wait_ge(mask_ready, i * NB + jb + 1)
                    if not (i is 0 and g is 0):
                        pe.wait_ge(copied, t - 1)
                    place = sc[:, u, :]
                    n = 0
                    for s, w in terms:
                        for d in range(DC):
                            last = nc.tensor.matmul(place, kT[s][:, d, bass.ts(tile, P)], q_in[:, i % 2, w, d, :],
                                                    start=(n == 0), stop=(n == 5))
                            if n == 0:
                                nc.tensor.matmul(place, neg_ident[:], mask8[:, r // 2, 2 * (r % 2) + u],
                                                 start=False, stop=False)
                            n += 1
                    last.then_inc(qk_done, 1)

            def attend(m, g, slot):
                pe.wait_ge(p_ready, m + 1)
                for u in range(2):
                    tile = 2 * g + u
                    first = g is 0 and u == 0
                    final = g is STEPS - 1 and u == 1
                    for e in range(E):
                        hi = p_hi[:, slot, u, e * P:(e + 1) * P]
                        lo = p_lo[:, slot, u, e * P:(e + 1) * P]
                        nc.tensor.matmul(acc[:, e, 0:D + 1], hi, v_hi[:, tile, 0:D + 1], start=first, stop=False)
                        nc.tensor.matmul(acc[:, e, 0:D], hi, v_lo[:, tile, :], start=False, stop=False)
                        last = nc.tensor.matmul(acc[:, e, 0:D + 1], lo, v_hi[:, tile, 0:D + 1], start=False,
                                                stop=final)
                last.then_inc(pv_done, 1)

            def turn_max(i):
                pe.wait_ge(colmax_ready, i + 1)
                for e in range(E):
                    last = nc.tensor.transpose(mc[:, e * P:(e + 1) * P], col_max[:, e * P:(e + 1) * P], ident[:])
                last.then_inc(maxT_done, 1)

            def spread_max(i):
                pe.wait_ge(diag_ready, i + 1)
                nc.tensor.matmul(mc, ones[:], diag_max.rearrange("p e q -> p (e q)"), start=True,
                                 stop=True).then_inc(max_spread, 1)

            def query_block(i, score, last_acc, this_acc):
                base = i * STEPS - LAG
                if score:
                    pe.wait_ge(q_loaded, 16 * (i + 1))
                    scores(i, 0, 0, 0)
                if this_acc:
                    turn_max(i - 1)
                if last_acc:
                    attend(base, STEPS - 2, 2)
                if this_acc:
                    spread_max(i - 1)
                if score:
                    scores(i, 1, 0, 1)
                if last_acc:
                    attend(base + 1, STEPS - 1, 3)
                if score:
                    scores(i, 2, 1, 2)
                if this_acc:
                    if last_acc:
                        pe.wait_ge(out_ready, i - 1)
                    attend(base + 2, 0, 0)
                if score:
                    scores(i, 3, 1, 3)
                if this_acc:
                    attend(base + 3, 1, 1)
                with pe.Fori(1, 4) as k:
                    for r in range(4):
                        if score:
                            scores(i, 4 * k + r, 2 * k + r // 2, r)
                        if this_acc:
                            attend(base + 4 * k + r, 4 * k + r - 2, (r + 2) % NP)

            pe.wait_ge(v_lo_s, NB + 1)
            query_block(0, True, False, False)
            query_block(1, True, False, True)
            with pe.Fori(2, NB) as i:
                query_block(i, True, True, True)
            query_block(NB, False, True, True)
            base = (NB + 1) * STEPS - LAG
            attend(base, STEPS - 2, 2)
            attend(base + 1, STEPS - 1, 3)


_INS = ["x", "adj", "W1", "b1", "W2", "b2", "WqT", "WkT", "WvT"]


def kernel(x, adj, L0_gnn_W1, L0_gnn_b1, L0_gnn_W2, L0_gnn_b2, L1_gnn_Wq, L1_gnn_Wk, L1_gnn_Wv):
    import numpy as np
    import concourse.bacc as bacc
    from concourse.bass_utils import run_bass_kernel_spmd

    arrays = dict(zip(_INS, (
        np.ascontiguousarray(x), np.ascontiguousarray(adj),
        np.ascontiguousarray(L0_gnn_W1), np.ascontiguousarray(L0_gnn_b1),
        np.ascontiguousarray(L0_gnn_W2), np.ascontiguousarray(L0_gnn_b2),
        np.ascontiguousarray(np.asarray(L1_gnn_Wq).T), np.ascontiguousarray(np.asarray(L1_gnn_Wk).T),
        np.ascontiguousarray(np.asarray(L1_gnn_Wv).T))))
    nc = bacc.Bacc("TRN2", target_bir_lowering=False, num_devices=1)
    args = [nc.dram_tensor(f"in_{n}", a.shape, mybir.dt.from_np(a.dtype), kind="ExternalInput").ap()
            for n, a in arrays.items()]
    out = nc.dram_tensor("out", (N, D), F32, kind="ExternalOutput").ap()
    two_layers(nc, *args, out)
    r = run_bass_kernel_spmd(nc, [{f"in_{n}": a for n, a in arrays.items()}], core_ids=[0])
    return r.results[0]["out"]
```

```python
from contextlib import ExitStack, contextmanager

import concourse.bass as bass
from concourse import mybir

ALU = mybir.AluOpType
ACT = mybir.ActivationFunctionType
AX = mybir.AxisListType
F32 = mybir.dt.float32
F16 = mybir.dt.float16
BF16 = mybir.dt.bfloat16
F8 = mybir.dt.float8e4
U8 = mybir.dt.uint8
U16 = mybir.dt.uint16
U32 = mybir.dt.uint32

P = 128
REGION = 141 * 1024
N = 4096
D = 256
HID = 512
F8_ONE = 56.0
PICK = 16
BLK = 512
NB = N // BLK
E = BLK // P
WORDS = N // 4
PAIRS = N // 2
DC = D // P
HC = HID // P
EPS = 1e-5
NEG = -1e30
FLOOR = -1e29
STEPS = 2 * NB
RING = STEPS + 2
LAG = STEPS + 3
NP = 4
NMASK = 4


class Order:

    def __init__(self, eng, sem):
        self.eng, self.sem, self.base, self.k = eng, sem, 0, 0

    def mark(self, ins):
        ins.then_inc(self.sem, 1)
        self.k += 1

    def wait(self):
        self.eng.wait_ge(self.sem, self.base + self.k)

    @contextmanager
    def loop(self, i, first, last, per):
        outer = self.base + self.k
        self.base, self.k = outer + (i - first) * per, 0
        yield
        assert self.k == per, (self.k, per)
        self.base, self.k = outer + (last - first) * per, 0


def two_layers(nc, x, adj, W1, b1, W2, b2, Wq, Wk, WvT, out):
    x_v = x.rearrange("(b p e) d -> b p e d", b=NB, e=E)
    out_v = out.rearrange("(b p e) d -> b p e d", b=NB, e=E)
    adj_v = adj.rearrange("(b p e) j -> b p e j", b=NB, e=E)
    x1_dram = nc.dram_tensor("x1_scratch", (NB, P, E, D), F32, kind="Internal").ap()
    q_dram = nc.dram_tensor("q_scratch", (NB, P, 2 * DC * BLK), F16, kind="Internal").ap()

    with ExitStack() as ctx:
        def sb(name, shape, dt):
            return ctx.enter_context(nc.sbuf_tensor(name, shape, dt))

        def sem(name):
            return ctx.enter_context(nc.semaphore(name))

        kT = [sb(f"kT_{s}", [P, DC, N], F16) for s in ("hi", "lo")]
        v_hi = sb("v_hi", [P, NB * E, D + 2], F16)
        v_lo = sb("v_lo", [P, NB * E, D], F16)
        ident = sb("ident", [P, P], F32)
        ident16 = sb("ident16", [P, P], F16)
        ones = sb("ones", [P, P], F32)
        eps_col = sb("eps_col", [P, 1], F32)

        region = sb("region", [P, REGION], U8)
        at = [0]

        def carve(shape, dt, size):
            n = size
            for s in shape:
                n *= s
            v = region[:, at[0]:at[0] + n].bitcast(dt)
            at[0] += n
            assert at[0] <= REGION, at[0]
            names = "abcd"[:len(shape)]
            if len(shape) > 1:
                v = v.rearrange("p (" + " ".join(names) + ") -> p " + " ".join(names),
                                **{m: s for m, s in zip(names, shape)})
            return v

        h_hi = carve([NB * E, D], F16, 2)
        h_lo = carve([NB * E, D], F16, 2)
        picked = carve([2, NB, BLK], U32, 4)
        picked8 = picked.bitcast(F8).rearrange("p a b (i e) -> p a b i e", e=4)
        picked16 = picked.bitcast(U16)
        rows = carve([E, N], U8, 1)
        count = carve([PAIRS + 2], F16, 2)
        w1 = [carve([DC, HID], F16, 2) for _ in range(2)]
        w2 = [carve([HC, D], F16, 2) for _ in range(2)]
        wq = [carve([DC, D], F16, 2) for _ in range(2)]
        wk = [carve([DC, D], F16, 2) for _ in range(2)]
        wqk = [carve([DC, D], F16, 2) for _ in range(2)]
        wv = [carve([DC, D], F16, 2) for _ in range(2)]
        hid_at = at[0]
        hid = [carve([DC, BLK], F16, 2) for _ in range(2)]
        act_f = carve([2, BLK], F32, 4)
        act_h = [carve([HC, BLK], F16, 2) for _ in range(2)]
        x1 = carve([E, D], F32, 4)
        h2 = carve([E, D], F32, 4)
        q_out = carve([2, DC, BLK], F16, 2)
        b1_col = carve([HC], F32, 4)
        b2_row = carve([D], F32, 4)
        b2_four = b2_row.unsqueeze(1).to_broadcast([P, E, D])
        falses = carve([PICK], F32, 4)
        false_n = carve([PICK], F32, 4)
        pad = carve([PICK], F32, 4)
        zeros = carve([PICK], F32, 4)
        need = carve([4], F32, 4)[:, 0:1]
        st6 = carve([3, E, 6], F32, 4)
        mean2 = carve([3, E], F32, 4)
        both = carve([3, E], F32, 4)
        apart = carve([3, E], F32, 4)
        var = carve([3, E], F32, 4)
        std = carve([3, E], F32, 4)
        rstd = carve([3, E], F32, 4)
        nbias = carve([3, E], F32, 4)
        x_in = [x1, h2]
        h_f = [act_f.rearrange("p a b -> p (a b)").rearrange("p (e d) -> p e d", e=E),
               region[:, hid_at:hid_at + 4096].bitcast(F32).rearrange("p (e d) -> p e d", e=E)]
        w_f = [act_h[0].rearrange("p a b -> p (a b)").bitcast(F32), act_h[1].rearrange("p a b -> p (a b)").bitcast(F32)]
        q_in = carve([2, 2, DC, BLK], F16, 2)
        at[0] = 0
        ring = carve([RING, 2, BLK], F32, 4)
        ring_tile = ring.rearrange("p g u i -> p (g u) i")
        adj_in = carve([NMASK, E, P], U32, 4)
        no_edge = adj_in.bitcast(U8).rearrange("p m t (i e) -> p m t e i", e=4)
        run_max = carve([2, BLK], F32, 4)
        p_hi = carve([NP, 2, BLK], F16, 2)
        p_lo = carve([NP, 2, BLK], F16, 2)
        p_f = carve([2, 2, BLK], F32, 4)
        col_max = carve([BLK], F32, 4)
        diag_max = carve([E, P], F32, 4)
        x1_in = carve([E, D], F32, 4)
        out_sb = carve([E, D], F32, 4)
        max_col = carve([E], F32, 4)
        den = carve([E], F32, 4)
        rden = carve([E], F32, 4)

        ps = ctx.enter_context(nc.psum_tensor("ps", [P, 8, BLK], F32))
        agg = ps[:, 0:2, :]
        tp = ps[:, 2:4, :]
        tp16 = tp.bitcast(U16)
        pa = ps[:, 4:8, :]
        wqk_ps = pa[:, 0, :].rearrange("p (a n) -> p a n", a=DC)
        sc = ps[:, 0:2, :]
        mc = ps[:, 3, :]
        acc = ps[:, 4:8, :]

        adj_loaded = [sem(f"adj_loaded{q}") for q in range(E)]
        x_loaded = [sem(f"x_loaded{i}") for i in range(2)]
        w_loaded = [sem(f"w_loaded{i}") for i in range(2)]
        b_loaded, xres_loaded, x1_stored, q_stored = sem("b_loaded"), sem("xres_loaded"), sem("x1_stored"), sem("q_stored")
        adj_in_loaded, q_loaded, x1_loaded, out_stored = sem("adj_in_loaded"), sem("q_loaded"), sem("x1_loaded"), sem("out_stored")
        consts_ready, w_split, pool_order, dve_order = sem("consts_ready"), sem("w_split"), sem("pool_order"), sem("dve_order")
        dve_consts = sem("dve_consts")
        ln0_stats, ln0_std, ln0_scale, ln0_h, h_hi_ready, h_ready = (sem(s) for s in (
            "ln0_stats", "ln0_std", "ln0_scale", "ln0_h", "h_hi_ready", "h_ready"))
        picks_ready, tp_ready, picks_stored = sem("picks_ready"), sem("tp_ready"), sem("picks_stored")
        agg_done, hid_hi, hid_lo = sem("agg_done"), sem("hid_hi"), sem("hid_lo")
        up_done, act_ready, act_lo = sem("up_done"), sem("act_ready"), sem("act_lo")
        down_done, xres_ready, x1_ready = sem("down_done"), sem("xres_ready"), sem("x1_ready")
        ln1_stats, ln1_std, ln1_scale, h2_ready = sem("ln1_stats"), sem("ln1_std"), sem("ln1_scale"), sem("h2_ready")
        h2T_done, h2T_hi, h2T_lo = sem("h2T_done"), sem("h2T_hi"), sem("h2T_lo")
        q_done, q_hi, q_lo = sem("q_done"), sem("q_hi"), sem("q_lo")
        qk_w_done, qk_w_hi, qk_w_lo = sem("qk_w_done"), sem("qk_w_hi"), sem("qk_w_lo")
        v_done, v_hi_s, v_lo_s = sem("v_done"), sem("v_hi_s"), sem("v_lo_s")
        qk_done, copied, maxed, colmax_ready, maxT_done = (sem(s) for s in (
            "qk_done", "copied", "maxed", "colmax_ready", "maxT_done"))
        diag_ready, max_spread, shifted, exp_done, p_ready = (sem(s) for s in (
            "diag_ready", "max_spread", "shifted", "exp_done", "p_ready"))
        flipped, pv_done, out_ready = sem("flipped"), sem("pv_done"), sem("out_ready")

        block = ctx.enter_context(nc.Block())


        @block.sync
        def _(sp):
            def load_rows(b, q):
                sp.dma_start(rows[:, q, :], adj_v[b, :, q, :]).then_inc(adj_loaded[q], 16)

            def load_x(c):
                if c >= 2:
                    sp.wait_ge(ln0_h, c - 1)
                sp.dma_start(x_in[c % 2], x_v[c]).then_inc(x_loaded[c % 2], 16)

            load_rows(0, 0)
            load_x(0)
            load_x(1)
            load_rows(0, 1)
            load_rows(0, 2)
            load_rows(0, 3)
            sp.dma_start(b1_col, b1.rearrange("(c p) -> p c", p=P),
                         allow_slow_non_contiguous=True).then_inc(b_loaded, 16)
            sp.dma_start(b2_row, b2.unsqueeze(0).to_broadcast([P, D])).then_inc(b_loaded, 16)
            for c in range(2, NB):
                load_x(c)

            def post_traffic(b):
                sp.wait_ge(x1_ready, b + 1)
                sp.dma_start(x1_dram[b], x1).then_inc(x1_stored, 16)
                sp.wait_ge(q_lo, b + 1)
                sp.dma_start(q_dram[b], q_out.rearrange("p s c i -> p (s c i)")).then_inc(q_stored, 16)
                sp.wait_ge(x1_stored, 16 * (b + 1))
                sp.wait_ge(q_stored, 16 * (b + 1))
                if b is not NB - 1:
                    sp.dma_start(x1, x_v[b + 1]).then_inc(xres_loaded, 16)

            sp.wait_ge(ln0_h, NB)
            sp.dma_start(x1, x_v[0]).then_inc(xres_loaded, 16)
            def load_q(i):
                if i is 1:
                    sp.wait_ge(q_loaded, 16)
                sp.dma_start(q_in[:, i % 2].rearrange("p s c i -> p (s c i)"), q_dram[i]).then_inc(q_loaded, 16)

            def load_x1(i):
                if i is 0:
                    sp.wait_ge(x1_stored, 16 * NB)
                else:
                    sp.wait_ge(out_stored, 16 * i)
                sp.dma_start(x1_in, x1_dram[i]).then_inc(x1_loaded, 16)

            def store_out(i):
                sp.wait_ge(out_ready, i + 1)
                sp.dma_start(out_v[i], out_sb).then_inc(out_stored, 16)

            with sp.Fori(0, NB - 2) as b:
                post_traffic(b)
            load_q(0)
            load_q(1)
            post_traffic(NB - 2)
            post_traffic(NB - 1)

            sp.wait_ge(v_lo_s, NB + 1)
            load_x1(0)
            with sp.Fori(2, NB) as i:
                sp.wait_ge(q_loaded, 16 * i)
                sp.wait_ge(qk_done, E * NB * (i - 1))
                load_q(i)
                store_out(i - 2)
                load_x1(i - 1)
            store_out(NB - 2)
            load_x1(NB - 1)
            store_out(NB - 1)
            sp.wait_ge(out_stored, 16 * NB)
            sp.wait_ge(x1_stored, 16 * NB)
            sp.wait_ge(q_stored, 16 * NB)

        @block.gpsimd
        def _(pool):
            order = Order(pool, pool_order)
            order.mark(nc.gpsimd.memset(ident[:], 0.0))
            order.mark(nc.gpsimd.memset(ident16[:], 0.0))
            order.wait()
            for t, val in ((ident, 1.0), (ident16, float(PICK))):
                nc.gpsimd.affine_select(out=t[:], in_=t[:], compare_op=ALU.not_equal, fill=val, base=0,
                                        pattern=[[-1, P]], channel_multiplier=1).then_inc(consts_ready, 1)
            nc.gpsimd.memset(ones[:], 1.0).then_inc(consts_ready, 1)
            nc.gpsimd.memset(v_hi[:, :, D:D + 1], 1.0).then_inc(consts_ready, 1)

            loads = ((W1.rearrange("(c p) n -> p c n", p=P), w1), (W2.rearrange("(c p) n -> p c n", p=P), w2),
                     (Wq.rearrange("(c p) n -> p c n", p=P), wq), (Wk.rearrange("(c p) n -> p c n", p=P), wk),
                     (WvT.rearrange("(c p) n -> p c n", p=P), wv))

            def load_w(n):
                src, w = loads[n]
                c = src.shape[1]
                dst = w_f[n % 2][:, 0:c * src.shape[2]].rearrange("p (c n) -> p c n", c=c)
                pool.dma_start(dst, src).then_inc(w_loaded[n % 2], 16)
                return dst

            def split_w(n, src):
                w = loads[n][1]
                pool.wait_ge(w_loaded[n % 2], 16 * (n // 2 + 1))
                order.mark(nc.gpsimd.tensor_copy(w[0], src))
                order.wait()
                nc.gpsimd.tensor_tensor(w[1], src, w[0], ALU.subtract).then_inc(w_split, 1)

            def split_h(c):
                pool.wait_ge(h_hi_ready, c + 1)
                nc.gpsimd.tensor_tensor(h_lo[:, c * E:(c + 1) * E, :], h_f[c % 2],
                                        h_hi[:, c * E:(c + 1) * E, :], ALU.subtract).then_inc(h_ready, 1)

            held = [load_w(0), load_w(1)]
            for c in range(NB):
                split_h(c)
            for n in range(len(loads)):
                split_w(n, held[n])
                if n + 2 < len(loads):
                    pool.wait_ge(w_split, n + 1)
                    held.append(load_w(n + 2))

            def post(b):
                pool.wait_ge(xres_loaded, 16 * (b + 1))
                nc.gpsimd.tensor_tensor(x1, x1, b2_four, ALU.add).then_inc(xres_ready, 1)
                for c in range(HC):
                    pool.wait_ge(act_ready, HC * b + c + 1)
                    nc.gpsimd.tensor_tensor(act_h[1][:, c, :], act_f[:, c % 2, :], act_h[0][:, c, :],
                                            ALU.subtract).then_inc(act_lo, 1)

            pool.wait_ge(b_loaded, 32)
            with pool.Fori(0, NB) as b:
                post(b)

            with pool.Fori(0, NB * STEPS // NP) as j:
                for slot in range(NP):
                    pool.wait_ge(exp_done, j * NP + slot + 1)
                    nc.gpsimd.tensor_tensor(p_lo[:, slot], p_f[:, slot % 2], p_hi[:, slot],
                                            ALU.subtract).then_inc(p_ready, 1)

        @block.vector
        def _(dve):
            order = Order(dve, dve_order)
            nc.vector.memset(eps_col[:], EPS).then_inc(dve_consts, 1)
            nc.vector.memset(need, 0.0).then_inc(v_lo_s, 1)
            order.mark(nc.vector.memset(zeros, 0.0))
            order.mark(nc.vector.memset(count[:, 0:1], 0.0))
            order.wait()

            def pieces(b, q):
                byte = rows[:, q, :].rearrange("p (w t) -> p w t", t=2)
                pick = rows[:, q, :].bitcast(F8).rearrange("p (w t) -> p w t", t=2)
                first16 = rows[:, q, 0:PICK]
                half = PAIRS // 2

                def count_first():
                    dve.wait_ge(adj_loaded[q], 16 * (b + 1))
                    order.mark(nc.vector.tensor_tensor_scan(count[:, 1:half + 1], byte[:, 0:half, 0],
                                                            byte[:, 0:half, 1], 0.0, ALU.add, ALU.add))
                    order.mark(nc.vector.tensor_scalar(falses, first16, -F8_ONE, F8_ONE, ALU.mult, ALU.add))

                def count_second():
                    order.wait()
                    order.mark(nc.vector.tensor_tensor_scan(count[:, half + 1:PAIRS + 1], byte[:, half:, 0],
                                                            byte[:, half:, 1], count[:, half:half + 1],
                                                            ALU.add, ALU.add))
                    order.mark(nc.vector.tensor_tensor_scan(false_n, falses, zeros, 0.0, ALU.add, ALU.add))
                    order.wait()

                def pick_odd():
                    order.mark(nc.vector.tensor_scalar(need, count[:, PAIRS:PAIRS + 1], -F8_ONE,
                                                       PICK * F8_ONE, ALU.mult, ALU.add))
                    order.mark(nc.vector.scalar_tensor_tensor(pick[:, :, 1], count[:, 1:PAIRS + 1], float(PICK),
                                                              byte[:, :, 1], ALU.is_le, ALU.mult, saturate=False))
                    order.wait()

                def pick_even():
                    order.mark(nc.vector.scalar_tensor_tensor(pad, false_n, need, falses, ALU.is_le, ALU.mult))
                    order.mark(nc.vector.scalar_tensor_tensor(pick[:, :, 0], count[:, 0:PAIRS], float(PICK - 1),
                                                              byte[:, :, 0], ALU.is_le, ALU.mult, saturate=False))
                    order.wait()
                    nc.vector.tensor_tensor(first16, first16, pad, ALU.add).then_inc(picks_ready, 1)

                return [count_first, count_second, pick_odd, pick_even]

            def stats(src, s):
                for e in range(E):
                    last = nc.vector.bn_stats(st6[:, s, e, :], src[:, e, :])
                order.mark(last)
                order.wait()
                even, odd = st6[:, s, :, 0:3], st6[:, s, :, 3:6]
                nc.vector.tensor_tensor(mean2[:, s, :], even[:, :, 1], odd[:, :, 1], ALU.add)
                nc.vector.tensor_tensor(both[:, s, :], even[:, :, 2], odd[:, :, 2], ALU.add)
                order.mark(nc.vector.tensor_tensor(apart[:, s, :], even[:, :, 1], odd[:, :, 1], ALU.subtract))
                order.wait()
                order.mark(nc.vector.tensor_tensor(apart[:, s, :], apart[:, s, :], apart[:, s, :], ALU.mult))
                order.wait()
                return nc.vector.scalar_tensor_tensor(var[:, s, :], apart[:, s, :], D / 4.0, both[:, s, :],
                                                      ALU.mult, ALU.add)

            def scale(s):
                order.mark(nc.vector.reciprocal(rstd[:, s, :], std[:, s, :]))
                order.wait()
                return nc.vector.scalar_tensor_tensor(nbias[:, s, :], mean2[:, s, :], -0.5, rstd[:, s, :],
                                                      ALU.mult, ALU.mult)

            def ln0_a(c):
                dve.wait_ge(x_loaded[c % 2], 16 * (c // 2 + 1))
                if c >= 2:
                    dve.wait_ge(ln0_h, c - 1)
                stats(x_in[c % 2], c % 2).then_inc(ln0_stats, 1)

            def ln0_b(c):
                dve.wait_ge(ln0_std, c + 1)
                scale(c % 2).then_inc(ln0_scale, 1)

            for j in range(4):
                ln0_a(2 * j)
                ln0_a(2 * j + 1)
                for n, piece in enumerate(pieces(0, j)):
                    piece()
                    if n < 2:
                        ln0_b(2 * j + n)
            def hid_low(b):
                dve.wait_ge(hid_hi, b + 1)
                nc.vector.scalar_tensor_tensor(hid[1], agg, 1.0 / PICK, hid[0], ALU.mult,
                                               ALU.subtract).then_inc(hid_lo, 1)

            def add_residual(b):
                dve.wait_ge(down_done, b + 1)
                dve.wait_ge(xres_ready, b + 1)
                nc.vector.tensor_tensor(x1, pa[:, 0:2, :].rearrange("p a (t d) -> p (a t) d", d=D), x1,
                                        ALU.add).then_inc(x1_ready, 1)
                dve.wait_ge(x1_ready, b + 1)
                stats(x1, 2).then_inc(ln1_stats, 1)

            def scale_h(b):
                dve.wait_ge(ln1_std, b + 1)
                scale(2).then_inc(ln1_scale, 1)

            def h_low(b):
                dve.wait_ge(h2T_hi, b + 1)
                nc.vector.tensor_tensor(kT[1][:, :, bass.ts(b, BLK)], pa[:, 2:4, :],
                                        kT[0][:, :, bass.ts(b, BLK)], ALU.subtract).then_inc(h2T_lo, 1)

            def q_low(b):
                dve.wait_ge(q_hi, b + 1)
                nc.vector.tensor_tensor(q_out[:, 1], pa[:, 0:2, :], q_out[:, 0], ALU.subtract).then_inc(q_lo, 1)

            def v_low(b):
                dve.wait_ge(v_hi_s, b + 1)
                nc.vector.tensor_tensor(v_lo[:, bass.ts(b, E), :],
                                        pa[:, 0:2, :].rearrange("p a (t d) -> p (a t) d", d=D),
                                        v_hi[:, bass.ts(b, E), 0:D], ALU.subtract).then_inc(v_lo_s, 1)

            def iteration(b, tiles):
                todo = [piece for tile in tiles for piece in pieces(*tile)]

                def run(n):
                    for _ in range(min(n, len(todo))):
                        todo.pop(0)()

                run(10)
                add_residual(b - 1)
                run(1)
                scale_h(b - 1)
                run(2)
                h_low(b - 1)
                run(2)
                q_low(b - 1)
                run(1)
                hid_low(b)
                v_low(b - 1)

            for piece in pieces(1, 0):
                piece()
            hid_low(0)
            for tile in ((1, 1), (1, 2), (1, 3), (2, 0)):
                for piece in pieces(*tile):
                    piece()
            dve.wait_ge(qk_w_hi, 1)
            nc.vector.tensor_tensor(wqk[1], wqk_ps, wqk[0], ALU.subtract).then_inc(qk_w_lo, 1)
            with dve.Fori(1, NB - 2) as b, order.loop(b, 1, NB - 2, 4 * 8 + 4):
                iteration(b, [(b + 1, 1), (b + 1, 2), (b + 1, 3), (b + 2, 0)])
            iteration(NB - 2, [(NB - 1, 1), (NB - 1, 2), (NB - 1, 3)])
            iteration(NB - 1, [])

            def add_mask(i, g, jb, r):
                n = i * STEPS + g
                if r % 2 == 0:
                    m = i * NB + jb
                    dve.wait_ge(adj_in_loaded, 16 * (m + 1))
                    slot = adj_in[:, jb % NMASK]
                    nc.vector.tensor_scalar(slot, slot, 0x01010101, 0, ALU.bitwise_xor,
                                            ALU.logical_shift_left).then_inc(flipped, 1)
                    dve.wait_ge(flipped, m + 1)
                if not (i is 0 or i is 1 and isinstance(g, int) and g < 2):
                    dve.wait_ge(exp_done, n - RING + 1)
                for u in range(2):
                    dve.wait_ge(qk_done, 2 * n + u + 1)
                    nc.vector.scalar_tensor_tensor(
                        ring_tile[:, n % RING * 2 + u, :].rearrange("p (e i) -> p e i", e=E),
                        no_edge[:, jb % NMASK, 2 * (r % 2) + u], NEG,
                        sc[:, u, :].rearrange("p (e i) -> p e i", e=E), ALU.mult, ALU.add).then_inc(copied, 1)

            def running_max(i, g):
                n = i * STEPS + g
                dve.wait_ge(copied, 2 * n + 2)
                if g is 1:
                    nc.vector.tensor_tensor(run_max, ring[:, (n + RING - 1) % RING], ring[:, n % RING],
                                            ALU.max).then_inc(maxed, 1)
                else:
                    dve.wait_ge(maxed, i * (STEPS - 1) + g - 1)
                    nc.vector.tensor_tensor(run_max, run_max, ring[:, n % RING], ALU.max).then_inc(maxed, 1)

            def column_max(i):
                dve.wait_ge(maxed, (i + 1) * (STEPS - 1))
                nc.vector.tensor_tensor(col_max, run_max[:, 0], run_max[:, 1], ALU.max).then_inc(colmax_ready, 1)

            def diagonal_max(i):
                dve.wait_ge(maxT_done, i + 1)
                order.mark(nc.vector.tensor_reduce(max_col, mc.rearrange("p (e q) -> p e q", e=E), axis=AX.X,
                                                   op=ALU.max))
                order.wait()
                order.mark(nc.vector.tensor_scalar(max_col, max_col, FLOOR, None, ALU.max))
                order.wait()
                nc.vector.tensor_tensor(diag_max, ident[:].unsqueeze(1).to_broadcast([P, E, P]),
                                        max_col.unsqueeze(2).to_broadcast([P, E, P]),
                                        ALU.mult).then_inc(diag_ready, 1)
                dve.wait_ge(max_spread, i + 1)

            def shift(i, g):
                place = ring[:, (i * STEPS + g + RING - STEPS) % RING]
                nc.vector.tensor_tensor(place, place, mc.unsqueeze(1).to_broadcast([P, 2, BLK]),
                                        ALU.subtract).then_inc(shifted, 1)

            def finish(i):
                dve.wait_ge(pv_done, (i + 1) * STEPS)
                order.mark(nc.vector.tensor_scalar(den, acc[:, :, D], 1e-30, None, ALU.max))
                order.wait()
                order.mark(nc.vector.reciprocal(rden, den))
                dve.wait_ge(x1_loaded, 16 * (i + 1))
                order.wait()
                for e in range(E):
                    last = nc.vector.scalar_tensor_tensor(out_sb[:, e, :], acc[:, e, 0:D], rden[:, e:e + 1],
                                                          x1_in[:, e, :], ALU.mult, ALU.add)
                last.then_inc(out_ready, 1)

            def step(i, g, jb, r, scores=True, probs=True, finishes=False):
                if finishes:
                    finish(i - 2)
                if g is 0:
                    if scores:
                        add_mask(i, g, jb, r)
                    if probs:
                        diagonal_max(i - 1)
                        shift(i, g)
                    return
                if probs:
                    shift(i, g)
                if scores:
                    add_mask(i, g, jb, r)
                    running_max(i, g)

            def query_block(i, scores, probs, finishes):
                for r in range(4):
                    step(i, r, r // 2, r, scores, probs, finishes and r == 3)
                with dve.Fori(1, 4) as k:
                    for r in range(4):
                        step(i, 4 * k + r, 2 * k + r // 2, r, scores, probs)
                if scores:
                    column_max(i)

            beside = {2: add_residual, 3: scale_h, 5: h_low, 7: q_low, 8: v_low}
            for g in range(STEPS):
                step(0, g, g // 2, g % 4, probs=False)
                if g in beside:
                    beside[g](NB - 1)
            dve.wait_ge(x1_stored, 16 * NB)
            dve.wait_ge(q_stored, 16 * NB)
            column_max(0)
            query_block(1, True, True, False)
            with dve.Fori(2, NB) as i, order.loop(i, 2, NB, 4):
                query_block(i, True, True, True)
            query_block(NB, False, True, True)
            finish(NB - 1)

        @block.scalar
        def _(act):
            act.wait_ge(dve_consts, 1)

            def ln0(c):
                act.wait_ge(ln0_stats, c + 1)
                nc.scalar.activation(std[:, c % 2, :], var[:, c % 2, :], ACT.Sqrt, scale=1.0 / D,
                                     bias=eps_col[:]).then_inc(ln0_std, 1)
                act.wait_ge(ln0_scale, c + 1)
                if c >= 2:
                    act.wait_ge(h_ready, c - 1)
                for e in range(E):
                    last = nc.scalar.activation(h_f[c % 2][:, e, :], x_in[c % 2][:, e, :], ACT.Relu,
                                                scale=rstd[:, c % 2, e:e + 1], bias=nbias[:, c % 2, e:e + 1])
                last.then_inc(ln0_h, 1)
                act.wait_ge(ln0_h, c + 1)
                nc.scalar.copy(h_hi[:, c * E:(c + 1) * E, :], h_f[c % 2]).then_inc(h_hi_ready, 1)

            def store_picks(b, q, h):
                act.wait_ge(tp_ready, 8 * b + 2 * q + h + 1)
                nc.scalar.copy(picked16[:, b % 2, 4 * h:4 * h + 4, 2 * P * q:2 * P * (q + 1)],
                               tp16[:, h, :].rearrange("p (c i) -> p c i", c=4)).then_inc(picks_stored, 1)

            def hid_high(b):
                act.wait_ge(agg_done, b + 1)
                nc.scalar.activation(hid[0], agg, ACT.Copy, scale=1.0 / PICK).then_inc(hid_hi, 1)

            def relu(b, c):
                act.wait_ge(up_done, HC * b + c + 1)
                if c >= 2:
                    act.wait_ge(act_lo, HC * b + c - 1)
                nc.scalar.activation(act_f[:, c % 2, :], pa[:, c, :], ACT.Relu, bias=b1_col[:, c:c + 1])
                nc.scalar.activation(act_h[0][:, c, :], pa[:, c, :], ACT.Relu,
                                     bias=b1_col[:, c:c + 1]).then_inc(act_ready, 1)

            def post_ops(b):
                def ups(c):
                    return lambda: (relu(b, c), relu(b, c + 1))

                def std_():
                    act.wait_ge(ln1_stats, b + 1)
                    nc.scalar.activation(std[:, 2, :], var[:, 2, :], ACT.Sqrt, scale=1.0 / D,
                                         bias=eps_col[:]).then_inc(ln1_std, 1)

                def norm():
                    act.wait_ge(ln1_scale, b + 1)
                    for e in range(E):
                        last = nc.scalar.activation(h2[:, e, :], x1[:, e, :], ACT.Relu,
                                                    scale=rstd[:, 2, e:e + 1], bias=nbias[:, 2, e:e + 1])
                    last.then_inc(h2_ready, 1)

                def turn():
                    act.wait_ge(h2T_done, b + 1)
                    nc.scalar.copy(kT[0][:, :, bass.ts(b, BLK)], pa[:, 2:4, :]).then_inc(h2T_hi, 1)

                def q_():
                    act.wait_ge(q_done, b + 1)
                    nc.scalar.copy(q_out[:, 0], pa[:, 0:2, :]).then_inc(q_hi, 1)

                def v_():
                    act.wait_ge(v_done, b + 1)
                    nc.scalar.copy(v_hi[:, bass.ts(b, E), 0:D],
                                   pa[:, 0:2, :].rearrange("p a (t d) -> p (a t) d", d=D)).then_inc(v_hi_s, 1)

                return {0: ups(0), 1: ups(2), 4: std_, 5: norm, 6: turn, 7: q_, 8: v_}

            def load_rows(b, q):
                act.dma_start(rows[:, q, :], adj_v[b, :, q, :]).then_inc(adj_loaded[q], 16)

            def load_mask(i, jb):
                if isinstance(jb, int) and jb >= NB:
                    i, jb = i + 1, jb - NB
                n = i * NB + jb
                early = i is 0 and isinstance(jb, int)
                if not (early and jb == 0):
                    act.wait_ge(adj_in_loaded, 16 * n)
                if not (early and jb < NMASK):
                    act.wait_ge(copied, E * (n - NMASK + 1))
                act.dma_start(adj_in[:, jb % NMASK].bitcast(U8),
                              adj_v[jb, :, :, bass.ts(i, BLK)]).then_inc(adj_in_loaded, 16)

            for c in range(NB):
                ln0(c)
                if c % 2:
                    store_picks(0, c // 2, 0)
                    store_picks(0, c // 2, 1)
                    load_rows(1, c // 2)
            act.wait_ge(b_loaded, 32)

            def iteration(b, turn, load, post, agg_too=True):
                ops = post_ops(b - 1) if post else {}
                for s in range(NB):
                    if turn:
                        store_picks(b + 1, s // 2, s % 2)
                        if load and s % 2:
                            load_rows(b + 2, s // 2)
                    if s in ops:
                        ops[s]()
                if agg_too:
                    hid_high(b)
                if post:
                    ops[NB]()

            hid_high(0)
            iteration(0, True, True, False, agg_too=False)
            act.wait_ge(qk_w_done, 1)
            nc.scalar.copy(wqk[0], wqk_ps).then_inc(qk_w_hi, 1)
            with act.Fori(1, NB - 2) as b:
                iteration(b, True, True, True)
            iteration(NB - 2, True, False, True)
            for jb in range(NMASK):
                load_mask(0, jb)
            iteration(NB - 1, False, False, True)
            ops = post_ops(NB - 1)
            for s, loads in ((0, ()), (1, ()), (4, (4,)), (5, (5,)), (6, ()), (7, (6, 7)), (8, (8, 9))):
                ops[s]()
                for jb in loads:
                    load_mask(0, jb)

            def probs(i, g, slot):
                m = (i - 1) * STEPS + g
                act.wait_ge(shifted, m + 1)
                if not (i is 1 and isinstance(g, int) and g < NP):
                    act.wait_ge(pv_done, m - NP + 1)
                if not (i is 1 and isinstance(g, int) and g < 2):
                    act.wait_ge(p_ready, m - 1)
                place = ring[:, (m % RING)]
                nc.scalar.activation(p_hi[:, slot], place, ACT.Exp)
                nc.scalar.activation(p_f[:, slot % 2], place, ACT.Exp).then_inc(exp_done, 1)

            def query_block(i, loads=True, more=True):
                for r in range(4):
                    probs(i, r, r)
                    if loads and r % 2 == 0:
                        load_mask(i, 2 + r // 2)
                with act.Fori(1, 3) as k:
                    for r in range(4):
                        probs(i, 4 * k + r, r)
                        if loads and r % 2 == 0:
                            load_mask(i, 2 * k + 2 + r // 2)
                for r in range(4):
                    probs(i, 12 + r, r)
                    if loads and more and r % 2 == 0:
                        load_mask(i, NB + r // 2)

            query_block(1)
            with act.Fori(2, NB - 1) as i:
                query_block(i)
            query_block(NB - 1, more=False)
            query_block(NB, loads=False)

        @block.tensor
        def _(pe):
            rows_w = rows.bitcast(F32)
            terms = ((0, 0), (0, 1), (1, 0))

            def turn_picks(b, q, h, first=False, summed=None):
                pe.wait_ge(picks_ready, E * b + q + 1)
                if not first:
                    pe.wait_ge(picks_stored, 8 * b + 2 * q + h - 1)
                for c in range(4):
                    if summed is not None and c == 3:
                        await_sum(summed)
                    w = (4 * h + c) * P
                    last = nc.tensor.transpose(tp[:, h, c * P:(c + 1) * P], rows_w[:, q, w:w + P], ident[:])
                last.then_inc(tp_ready, 1)

            def await_sum(b):
                if b is not 0:
                    pe.wait_ge(hid_lo, b)
                pe.wait_ge(picks_stored, 8 * (b + 1))

            def sum_picks(b, c, par, q=None):
                cols = slice(0, BLK) if q is None else slice(q * P, (q + 1) * P)
                if b is 0:
                    pe.wait_ge(h_ready, c + 1)
                for e in range(E):
                    for half in (h_hi, h_lo):
                        for d in range(DC):
                            nc.tensor.matmul(agg[:, d, cols], half[:, c * E + e, d * P:(d + 1) * P],
                                             picked8[:, par, c, cols, e],
                                             start=(c == 0 and e == 0 and half is h_hi and q in (None, 0)),
                                             stop=False, skip_group_check=q is not None)
                if c == NB - 1 and q in (None, E - 1):
                    for e in range(E):
                        for half in (h_hi, h_lo):
                            for d in range(DC):
                                last = nc.tensor.matmul(agg[:, d, e * P:(e + 1) * P],
                                                        half[:, b * E + e, d * P:(d + 1) * P], ident16[:],
                                                        start=False, stop=(e == E - 1 and half is h_lo),
                                                        skip_group_check=q is not None)
                    last.then_inc(agg_done, 1)

            def up(b, c):
                n = 0
                for s, t in terms:
                    for d in range(DC):
                        last = nc.tensor.matmul(pa[:, c, :], w1[s][:, d, c * P:(c + 1) * P], hid[t][:, d, :],
                                                start=(n == 0), stop=(n == 5))
                        n += 1
                last.then_inc(up_done, 1)

            def down(b):
                pe.wait_ge(act_lo, HC * (b + 1))
                for e in range(E):
                    n = 0
                    for s, t in terms:
                        for c in range(HC):
                            last = nc.tensor.matmul(pa[:, e // 2, (e % 2) * D:(e % 2 + 1) * D],
                                                    act_h[s][:, c, e * P:(e + 1) * P], w2[t][:, c, :],
                                                    start=(n == 0), stop=(n == 11))
                            n += 1
                last.then_inc(down_done, 1)

            def turn_h2(b):
                pe.wait_ge(h2_ready, b + 1)
                for d in range(DC):
                    for e in range(E):
                        last = nc.tensor.transpose(pa[:, 2 + d, e * P:(e + 1) * P], h2[:, e, d * P:(d + 1) * P],
                                                   ident[:])
                last.then_inc(h2T_done, 1)

            def project_q(b):
                pe.wait_ge(h2T_lo, b + 1)
                for d in range(DC):
                    n = 0
                    for s, t in terms:
                        for c in range(DC):
                            last = nc.tensor.matmul(pa[:, d, :], wqk[s][:, c, d * P:(d + 1) * P],
                                                    kT[t][:, c, bass.ts(b, BLK)], start=(n == 0), stop=(n == 5))
                            n += 1
                last.then_inc(q_done, 1)

            def project_v(b):
                pe.wait_ge(q_lo, b + 1)
                for e in range(E):
                    n = 0
                    for s, t in terms:
                        for c in range(DC):
                            last = nc.tensor.matmul(pa[:, e // 2, (e % 2) * D:(e % 2 + 1) * D],
                                                    kT[s][:, c, bass.ds(b * BLK + e * P, P)], wv[t][:, c, :],
                                                    start=(n == 0), stop=(n == 5))
                            n += 1
                last.then_inc(v_done, 1)

            def post_stage(b, s):
                if s == 0:
                    pe.wait_ge(hid_lo, b + 1)
                    pe.wait_ge(v_lo_s, b + 1)
                    up(b, 0)
                    up(b, 1)
                if s == 1:
                    up(b, 2)
                    up(b, 3)
                if s == 3:
                    down(b)
                if s == 5:
                    turn_h2(b)
                if s == 6:
                    project_q(b)
                if s == 7:
                    project_v(b)

            def weight_product():
                for a in range(DC):
                    n = 0
                    for s, t in terms:
                        for c in range(DC):
                            last = nc.tensor.matmul(wqk_ps[:, a, :], wq[s][:, c, a * P:(a + 1) * P], wk[t][:, c, :],
                                                    start=(n == 0), stop=(n == 5))
                            n += 1
                last.then_inc(qk_w_done, 1)

            def iteration(b, par, turn):
                for s in range(NB):
                    if turn:
                        turn_picks(b + 1, s // 2, s % 2, summed=b if s == 0 else None)
                    elif s == 0:
                        await_sum(b)
                    sum_picks(b, s, par)
                    post_stage(b - 1, s)

            pe.wait_ge(consts_ready, 4)
            for q in range(E):
                for h in range(2):
                    turn_picks(0, q, h, first=q == 0)
                pe.wait_ge(picks_stored, 2 * q + 2)
                for c in range(2 * q):
                    sum_picks(0, c, 0, q)
                for c in (2 * q, 2 * q + 1):
                    for t in range(q + 1):
                        sum_picks(0, c, 0, t)
            for q in range(E):
                for h in range(2):
                    turn_picks(1, q, h)
            pe.wait_ge(w_split, 5)
            weight_product()
            pe.wait_ge(qk_w_lo, 1)
            with pe.Fori(0, NB // 2 - 1) as j:
                iteration(2 * j + 1, 1, True)
                iteration(2 * j + 2, 0, True)
            iteration(NB - 1, 1, False)

            def scores(i, g):
                for u in range(2):
                    tile = 2 * g + u
                    if not (i is 0 and g is 0):
                        pe.wait_ge(copied, i * STEPS * 2 + tile - 1)
                    n = 0
                    for s, w in terms:
                        for d in range(DC):
                            last = nc.tensor.matmul(sc[:, u, :], kT[s][:, d, bass.ts(tile, P)], q_in[:, i % 2, w, d, :],
                                                    start=(n == 0), stop=(n == 5))
                            n += 1
                    last.then_inc(qk_done, 1)

            def attend(m, g, slot):
                pe.wait_ge(p_ready, m + 1)
                for u in range(2):
                    tile = 2 * g + u
                    first = g is 0 and u == 0
                    final = g is STEPS - 1 and u == 1
                    for e in range(E):
                        hi = p_hi[:, slot, u, e * P:(e + 1) * P]
                        lo = p_lo[:, slot, u, e * P:(e + 1) * P]
                        nc.tensor.matmul(acc[:, e, 0:D + 1], hi, v_hi[:, tile, 0:D + 1], start=first, stop=False)
                        nc.tensor.matmul(acc[:, e, 0:D], hi, v_lo[:, tile, :], start=False, stop=False)
                        last = nc.tensor.matmul(acc[:, e, 0:D + 1], lo, v_hi[:, tile, 0:D + 1], start=False,
                                                stop=final)
                last.then_inc(pv_done, 1)

            def turn_max(i):
                pe.wait_ge(colmax_ready, i + 1)
                for e in range(E):
                    last = nc.tensor.transpose(mc[:, e * P:(e + 1) * P], col_max[:, e * P:(e + 1) * P], ident[:])
                last.then_inc(maxT_done, 1)

            def spread_max(i):
                pe.wait_ge(diag_ready, i + 1)
                nc.tensor.matmul(mc, ones[:], diag_max.rearrange("p e q -> p (e q)"), start=True,
                                 stop=True).then_inc(max_spread, 1)

            def query_block(i, score, last_acc):
                base = i * STEPS - LAG
                if score:
                    pe.wait_ge(q_loaded, 16 * (i + 1))
                    scores(i, 0)
                turn_max(i - 1)
                if last_acc:
                    attend(base, 13, 1)
                spread_max(i - 1)
                for r in (1, 2):
                    if score:
                        scores(i, r)
                    if last_acc:
                        attend(base + r, 13 + r, 1 + r)
                if score:
                    scores(i, 3)
                if last_acc:
                    pe.wait_ge(out_ready, i - 1)
                attend(base + 3, 0, 0)
                with pe.Fori(1, 4) as k:
                    for r in range(4):
                        if score:
                            scores(i, 4 * k + r)
                        attend(base + 4 * k + r, 4 * k + r - 3, (r + 1) % NP)

            pe.wait_ge(q_loaded, 16)
            stages = {0: 0, 1: 1, 3: 3, 6: 5, 8: 6, 9: 7}
            for g in range(STEPS):
                if g in stages:
                    post_stage(NB - 1, stages[g])
                scores(0, g)
            pe.wait_ge(v_lo_s, NB + 1)
            query_block(1, True, False)
            with pe.Fori(2, NB) as i:
                query_block(i, True, True)
            query_block(NB, False, True)
            base = (NB + 1) * STEPS - LAG
            for r in range(3):
                attend(base + r, 13 + r, 1 + r)


_INS = ["x", "adj", "W1", "b1", "W2", "b2", "Wq", "Wk", "WvT"]


def kernel(x, adj, L0_gnn_W1, L0_gnn_b1, L0_gnn_W2, L0_gnn_b2, L1_gnn_Wq, L1_gnn_Wk, L1_gnn_Wv):
    import numpy as np
    import concourse.bacc as bacc
    from concourse.bass_utils import run_bass_kernel_spmd

    arrays = dict(zip(_INS, (
        np.ascontiguousarray(x), np.ascontiguousarray(adj),
        np.ascontiguousarray(L0_gnn_W1), np.ascontiguousarray(L0_gnn_b1),
        np.ascontiguousarray(L0_gnn_W2), np.ascontiguousarray(L0_gnn_b2),
        np.ascontiguousarray(L1_gnn_Wq), np.ascontiguousarray(L1_gnn_Wk),
        np.ascontiguousarray(np.asarray(L1_gnn_Wv).T))))
    nc = bacc.Bacc("TRN2", target_bir_lowering=False, num_devices=1)
    args = [nc.dram_tensor(f"in_{n}", a.shape, mybir.dt.from_np(a.dtype), kind="ExternalInput").ap()
            for n, a in arrays.items()]
    out = nc.dram_tensor("out", (N, D), F32, kind="ExternalOutput").ap()
    two_layers(nc, *args, out)
    r = run_bass_kernel_spmd(nc, [{f"in_{n}": a for n, a in arrays.items()}], core_ids=[0])
    return r.results[0]["out"]
```

```python
from contextlib import ExitStack, contextmanager

import concourse.bass as bass
from concourse import mybir

ALU = mybir.AluOpType
ACT = mybir.ActivationFunctionType
AX = mybir.AxisListType
F32 = mybir.dt.float32
F16 = mybir.dt.float16
F8 = mybir.dt.float8e4
U8 = mybir.dt.uint8
U16 = mybir.dt.uint16
U32 = mybir.dt.uint32

P = 128
REGION = 141 * 1024
N = 4096
D = 256
HID = 512
F8_ONE = 56.0
PICK = 16
BLK = 512
NB = N // BLK
E = BLK // P
PAIRS = N // 2
DC = D // P
HC = HID // P
EPS = 1e-5
NEG = -1e30
FLOOR = -1e29
STEPS = 2 * NB
RING = STEPS + 2
LAG = STEPS + 3
NP = 4
LN = 4
NMASK = 4


class Order:

    def __init__(self, eng, sem):
        self.eng, self.sem, self.base, self.k = eng, sem, 0, 0

    def mark(self, ins):
        ins.then_inc(self.sem, 1)
        self.k += 1

    def wait(self):
        self.eng.wait_ge(self.sem, self.base + self.k)

    @contextmanager
    def loop(self, i, first, last, per):
        outer = self.base + self.k
        self.base, self.k = outer + (i - first) * per, 0
        yield
        assert self.k == per, (self.k, per)
        self.base, self.k = outer + (last - first) * per, 0


def two_layers(nc, x, adj, W1, b1, W2, b2, Wq, Wk, WvT, out):
    x_v = x.rearrange("(b p e) d -> b p e d", b=NB, e=E)
    out_v = out.rearrange("(b p e) d -> b p e d", b=NB, e=E)
    adj_v = adj.rearrange("(b p e) j -> b p e j", b=NB, e=E)
    x1_dram = nc.dram_tensor("x1_scratch", (NB, P, E, D), F32, kind="Internal").ap()
    q_dram = nc.dram_tensor("q_scratch", (NB, P, 2 * DC * BLK), F16, kind="Internal").ap()

    with ExitStack() as ctx:
        def sb(name, shape, dt):
            return ctx.enter_context(nc.sbuf_tensor(name, shape, dt))

        def sem(name):
            return ctx.enter_context(nc.semaphore(name))

        kT = [sb(f"kT_{s}", [P, DC, N], F16) for s in ("hi", "lo")]
        v_hi = sb("v_hi", [P, NB * E, D + 2], F16)
        v_lo = sb("v_lo", [P, NB * E, D], F16)
        ident = sb("ident", [P, P], F32)
        ident16 = sb("ident16", [P, P], F16)
        ones = sb("ones", [P, P], F32)
        eps_col = sb("eps_col", [P, 1], F32)

        region = sb("region", [P, REGION], U8)
        at = [0]

        def carve(shape, dt, size):
            n = size
            for s in shape:
                n *= s
            v = region[:, at[0]:at[0] + n].bitcast(dt)
            at[0] += n
            assert at[0] <= REGION, at[0]
            names = "abcd"[:len(shape)]
            if len(shape) > 1:
                v = v.rearrange("p (" + " ".join(names) + ") -> p " + " ".join(names),
                                **{m: s for m, s in zip(names, shape)})
            return v

        h_hi = carve([NB * E, D], F16, 2)
        h_lo = carve([NB * E, D], F16, 2)
        picked = carve([2, NB, BLK], U32, 4)
        picked8 = picked.bitcast(F8).rearrange("p a b (i e) -> p a b i e", e=4)
        picked16 = picked.bitcast(U16)
        rows = carve([E, N], U8, 1)
        count = carve([PAIRS + 2], F16, 2)
        w1 = [carve([DC, HID], F16, 2) for _ in range(2)]
        w2 = [carve([HC, D], F16, 2) for _ in range(2)]
        wq = [carve([DC, D], F16, 2) for _ in range(2)]
        wk = [carve([DC, D], F16, 2) for _ in range(2)]
        wqk = [carve([DC, D], F16, 2) for _ in range(2)]
        wv = [carve([DC, D], F16, 2) for _ in range(2)]
        hid_at = at[0]
        hid = [carve([DC, BLK], F16, 2) for _ in range(2)]
        act_f = carve([2, BLK], F32, 4)
        act_h = [carve([HC, BLK], F16, 2) for _ in range(2)]
        x1 = carve([E, D], F32, 4)
        h2 = carve([E, D], F32, 4)
        q_out = carve([2, DC, BLK], F16, 2)
        b1_col = carve([HC], F32, 4)
        b2_row = carve([D], F32, 4)
        b2_four = b2_row.unsqueeze(1).to_broadcast([P, E, D])
        falses = carve([PICK], F32, 4)
        false_n = carve([PICK], F32, 4)
        pad = carve([PICK], F32, 4)
        zeros = carve([PICK], F32, 4)
        need = carve([4], F32, 4)[:, 0:1]
        st6 = carve([LN + 1, E, 6], F32, 4)
        mean2 = carve([LN + 1, E], F32, 4)
        both = carve([LN + 1, E], F32, 4)
        apart = carve([LN + 1, E], F32, 4)
        var = carve([LN + 1, E], F32, 4)
        std = carve([LN + 1, E], F32, 4)
        rstd = carve([LN + 1, E], F32, 4)
        nbias = carve([LN + 1, E], F32, 4)
        x_in = [kT[c // LN][:].rearrange("p c n -> p (c n)").bitcast(F32).rearrange(
            "p (b e d) -> p b e d", b=LN, e=E)[:, c % LN] for c in range(NB)]
        h_f = [v_lo[:].rearrange("p t d -> p (t d)").bitcast(F32).rearrange(
            "p (b e d) -> p b e d", b=LN, e=E)[:, c] for c in range(LN)]
        w_f = [act_h[0].rearrange("p a b -> p (a b)").bitcast(F32), act_h[1].rearrange("p a b -> p (a b)").bitcast(F32)]
        q_in = carve([2, 2, DC, BLK], F16, 2)
        at[0] = 0
        ring = carve([RING, 2, BLK], F32, 4)
        ring_tile = ring.rearrange("p g u i -> p (g u) i")
        adj_in = carve([NMASK, E, P], U32, 4)
        no_edge = adj_in.bitcast(U8).rearrange("p m t (i e) -> p m t e i", e=4)
        run_max = carve([2, BLK], F32, 4)
        p_hi = carve([NP, 2, BLK], F16, 2)
        p_lo = carve([NP, 2, BLK], F16, 2)
        p_f = carve([2, 2, BLK], F32, 4)
        col_max = carve([BLK], F32, 4)
        diag_max = carve([E, P], F32, 4)
        x1_in = carve([E, D], F32, 4)
        out_sb = carve([E, D], F32, 4)
        max_col = carve([E], F32, 4)
        den = carve([E], F32, 4)
        rden = carve([E], F32, 4)

        ps = ctx.enter_context(nc.psum_tensor("ps", [P, 8, BLK], F32))
        agg = ps[:, 0:2, :]
        tp = ps[:, 2:4, :]
        tp16 = tp.bitcast(U16)
        pa = ps[:, 4:8, :]
        wqk_ps = pa[:, 0, :].rearrange("p (a n) -> p a n", a=DC)
        sc = ps[:, 0:4, :]
        mc = ps[:, 3, :]
        acc = ps[:, 4:8, :]

        adj_loaded = [sem(f"adj_loaded{q}") for q in range(E)]
        x_loaded = [sem(f"x_loaded{i}") for i in range(NB)]
        w_loaded = [sem(f"w_loaded{i}") for i in range(2)]
        b_loaded, xres_loaded, x1_stored, q_stored = sem("b_loaded"), sem("xres_loaded"), sem("x1_stored"), sem("q_stored")
        adj_in_loaded, q_loaded, x1_loaded, out_stored = sem("adj_in_loaded"), sem("q_loaded"), sem("x1_loaded"), sem("out_stored")
        consts_ready, w_split, pool_order, dve_order = sem("consts_ready"), sem("w_split"), sem("pool_order"), sem("dve_order")
        dve_consts = sem("dve_consts")
        ln0_stats, ln0_std, ln0_scale, ln0_h, h_hi_ready, h_ready = (sem(s) for s in (
            "ln0_stats", "ln0_std", "ln0_scale", "ln0_h", "h_hi_ready", "h_ready"))
        picks_ready, tp_ready, picks_stored = sem("picks_ready"), sem("tp_ready"), sem("picks_stored")
        agg_done, hid_hi, hid_lo = sem("agg_done"), sem("hid_hi"), sem("hid_lo")
        up_done, act_ready, act_lo = sem("up_done"), sem("act_ready"), sem("act_lo")
        down_done, xres_ready, x1_ready = sem("down_done"), sem("xres_ready"), sem("x1_ready")
        ln1_stats, ln1_std, ln1_scale, h2_ready = sem("ln1_stats"), sem("ln1_std"), sem("ln1_scale"), sem("h2_ready")
        h2T_done, h2T_hi, h2T_lo = sem("h2T_done"), sem("h2T_hi"), sem("h2T_lo")
        q_done, q_hi, q_lo = sem("q_done"), sem("q_hi"), sem("q_lo")
        qk_w_done, qk_w_hi, qk_w_lo = sem("qk_w_done"), sem("qk_w_hi"), sem("qk_w_lo")
        v_done, v_hi_s, v_lo_s = sem("v_done"), sem("v_hi_s"), sem("v_lo_s")
        qk_done, copied, maxed, colmax_ready, maxT_done = (sem(s) for s in (
            "qk_done", "copied", "maxed", "colmax_ready", "maxT_done"))
        diag_ready, max_spread, shifted, exp_done, p_ready = (sem(s) for s in (
            "diag_ready", "max_spread", "shifted", "exp_done", "p_ready"))
        flipped, pv_done, out_ready = sem("flipped"), sem("pv_done"), sem("out_ready")

        block = ctx.enter_context(nc.Block())


        @block.sync
        def _(sp):
            def load_rows(b, q):
                sp.dma_start(rows[:, q, :], adj_v[b, :, q, :]).then_inc(adj_loaded[q], 16)

            def load_x(c):
                sp.dma_start(x_in[c], x_v[c]).then_inc(x_loaded[c], 16)

            load_rows(0, 0)
            load_x(0)
            load_x(1)
            load_x(2)
            load_x(3)
            load_rows(0, 1)
            for c in range(4, NB):
                load_x(c)
            load_rows(0, 2)
            load_rows(0, 3)
            sp.dma_start(b1_col, b1.rearrange("(c p) -> p c", p=P),
                         allow_slow_non_contiguous=True).then_inc(b_loaded, 16)
            sp.dma_start(b2_row, b2.unsqueeze(0).to_broadcast([P, D])).then_inc(b_loaded, 16)
            sp.dma_start(x1, x_v[0]).then_inc(xres_loaded, 16)

            def post_traffic(b):
                sp.wait_ge(x1_ready, b + 1)
                sp.dma_start(x1_dram[b], x1).then_inc(x1_stored, 16)
                sp.wait_ge(q_lo, b + 1)
                sp.dma_start(q_dram[b], q_out.rearrange("p s c i -> p (s c i)")).then_inc(q_stored, 16)
                sp.wait_ge(x1_stored, 16 * (b + 1))
                sp.wait_ge(q_stored, 16 * (b + 1))
                if b is not NB - 1:
                    sp.dma_start(x1, x_v[b + 1]).then_inc(xres_loaded, 16)

            def load_q(i):
                if i is 1:
                    sp.wait_ge(q_loaded, 16)
                sp.dma_start(q_in[:, i % 2].rearrange("p s c i -> p (s c i)"), q_dram[i]).then_inc(q_loaded, 16)

            def load_x1(i):
                if i is 0:
                    sp.wait_ge(x1_stored, 16 * NB)
                else:
                    sp.wait_ge(out_stored, 16 * i)
                sp.dma_start(x1_in, x1_dram[i]).then_inc(x1_loaded, 16)

            def store_out(i):
                sp.wait_ge(out_ready, i + 1)
                sp.dma_start(out_v[i], out_sb).then_inc(out_stored, 16)

            with sp.Fori(0, NB - 2) as b:
                post_traffic(b)
            load_q(0)
            load_q(1)
            post_traffic(NB - 2)
            post_traffic(NB - 1)

            sp.wait_ge(v_lo_s, NB + 1)
            load_x1(0)
            with sp.Fori(2, NB) as i:
                sp.wait_ge(q_loaded, 16 * i)
                sp.wait_ge(qk_done, E * NB * (i - 1))
                load_q(i)
                store_out(i - 2)
                load_x1(i - 1)
            store_out(NB - 2)
            load_x1(NB - 1)
            store_out(NB - 1)
            sp.wait_ge(out_stored, 16 * NB)
            sp.wait_ge(x1_stored, 16 * NB)
            sp.wait_ge(q_stored, 16 * NB)

        @block.gpsimd
        def _(pool):
            order = Order(pool, pool_order)
            order.mark(nc.gpsimd.memset(ident[:], 0.0))
            order.mark(nc.gpsimd.memset(ident16[:], 0.0))
            order.wait()
            for t, val in ((ident, 1.0), (ident16, float(PICK))):
                nc.gpsimd.affine_select(out=t[:], in_=t[:], compare_op=ALU.not_equal, fill=val, base=0,
                                        pattern=[[-1, P]], channel_multiplier=1).then_inc(consts_ready, 1)
            nc.gpsimd.memset(ones[:], 1.0).then_inc(consts_ready, 1)
            nc.gpsimd.memset(v_hi[:, :, D:D + 1], 1.0).then_inc(consts_ready, 1)

            loads = ((W1.rearrange("(c p) n -> p c n", p=P), w1), (W2.rearrange("(c p) n -> p c n", p=P), w2),
                     (Wq.rearrange("(c p) n -> p c n", p=P), wq), (Wk.rearrange("(c p) n -> p c n", p=P), wk),
                     (WvT.rearrange("(c p) n -> p c n", p=P), wv))

            def staged(n):
                c, width = loads[n][0].shape[1:]
                return w_f[n % 2][:, 0:c * width].rearrange("p (c n) -> p c n", c=c)

            def load_w(n):
                pool.dma_start(staged(n), loads[n][0]).then_inc(w_loaded[n % 2], 16)

            def split_w(n):
                src, w = staged(n), loads[n][1]
                pool.wait_ge(w_loaded[n % 2], 16 * (n // 2 + 1))
                order.mark(nc.gpsimd.tensor_copy(w[0], src))
                order.wait()
                nc.gpsimd.tensor_tensor(w[1], src, w[0], ALU.subtract).then_inc(w_split, 1)

            def split_h(c):
                pool.wait_ge(h_hi_ready, c + 1)
                nc.gpsimd.tensor_tensor(h_lo[:, c * E:(c + 1) * E, :], h_f[c % LN],
                                        h_hi[:, c * E:(c + 1) * E, :], ALU.subtract).then_inc(h_ready, 1)

            for c in range(NB):
                split_h(c)
                if c == 1:
                    load_w(0)
                    load_w(1)
                for n in {5: (0,), 6: (1,), 7: (2, 3, 4)}.get(c, ()):
                    split_w(n)
                    if n + 2 < len(loads):
                        pool.wait_ge(w_split, n + 1)
                        load_w(n + 2)

            def post(b):
                pool.wait_ge(xres_loaded, 16 * (b + 1))
                nc.gpsimd.tensor_tensor(x1, x1, b2_four, ALU.add).then_inc(xres_ready, 1)
                for c in range(HC):
                    pool.wait_ge(act_ready, HC * b + c + 1)
                    nc.gpsimd.tensor_tensor(act_h[1][:, c, :], act_f[:, c % 2, :], act_h[0][:, c, :],
                                            ALU.subtract).then_inc(act_lo, 1)

            pool.wait_ge(b_loaded, 32)
            with pool.Fori(0, NB) as b:
                post(b)

            with pool.Fori(0, NB * STEPS // NP) as j:
                for slot in range(NP):
                    pool.wait_ge(exp_done, j * NP + slot + 1)
                    nc.gpsimd.tensor_tensor(p_lo[:, slot], p_f[:, slot % 2], p_hi[:, slot],
                                            ALU.subtract).then_inc(p_ready, 1)

        @block.vector
        def _(dve):
            order = Order(dve, dve_order)
            nc.vector.memset(eps_col[:], EPS).then_inc(dve_consts, 1)
            nc.vector.memset(need, 0.0).then_inc(v_lo_s, 1)
            order.mark(nc.vector.memset(zeros, 0.0))
            order.mark(nc.vector.memset(count[:, 0:1], 0.0))
            order.wait()

            def piece(b, q, n):
                byte = rows[:, q, :].rearrange("p (w t) -> p w t", t=2)
                pick = rows[:, q, :].bitcast(F8).rearrange("p (w t) -> p w t", t=2)
                first16 = rows[:, q, 0:PICK]
                half = PAIRS // 2
                if n == 0:
                    dve.wait_ge(adj_loaded[q], 16 * (b + 1))
                    order.mark(nc.vector.tensor_tensor_scan(count[:, 1:half + 1], byte[:, 0:half, 0],
                                                            byte[:, 0:half, 1], 0.0, ALU.add, ALU.add))
                    order.mark(nc.vector.tensor_scalar(falses, first16, -F8_ONE, F8_ONE, ALU.mult, ALU.add))
                if n == 1:
                    order.wait()
                    order.mark(nc.vector.tensor_tensor_scan(count[:, half + 1:PAIRS + 1], byte[:, half:, 0],
                                                            byte[:, half:, 1], count[:, half:half + 1],
                                                            ALU.add, ALU.add))
                    order.mark(nc.vector.tensor_tensor_scan(false_n, falses, zeros, 0.0, ALU.add, ALU.add))
                    order.wait()
                if n == 2:
                    order.mark(nc.vector.tensor_scalar(need, count[:, PAIRS:PAIRS + 1], -F8_ONE,
                                                       PICK * F8_ONE, ALU.mult, ALU.add))
                    order.mark(nc.vector.scalar_tensor_tensor(pick[:, :, 1], count[:, 1:PAIRS + 1], float(PICK),
                                                              byte[:, :, 1], ALU.is_le, ALU.mult, saturate=False))
                    order.wait()
                if n == 3:
                    order.mark(nc.vector.scalar_tensor_tensor(pad, false_n, need, falses, ALU.is_le, ALU.mult))
                    order.mark(nc.vector.scalar_tensor_tensor(pick[:, :, 0], count[:, 0:PAIRS], float(PICK - 1),
                                                              byte[:, :, 0], ALU.is_le, ALU.mult, saturate=False))
                    order.wait()
                    nc.vector.tensor_tensor(first16, first16, pad, ALU.add).then_inc(picks_ready, 1)

            def picks(b, first, last):
                for m in range(first, last):
                    piece(b + m // (4 * E), m // 4 % E, m % 4)

            def stats(src, s):
                for e in range(E):
                    last = nc.vector.bn_stats(st6[:, s, e, :], src[:, e, :])
                order.mark(last)
                order.wait()
                even, odd = st6[:, s, :, 0:3], st6[:, s, :, 3:6]
                nc.vector.tensor_tensor(mean2[:, s, :], even[:, :, 1], odd[:, :, 1], ALU.add)
                nc.vector.tensor_tensor(both[:, s, :], even[:, :, 2], odd[:, :, 2], ALU.add)
                order.mark(nc.vector.tensor_tensor(apart[:, s, :], even[:, :, 1], odd[:, :, 1], ALU.subtract))
                order.wait()
                order.mark(nc.vector.tensor_tensor(apart[:, s, :], apart[:, s, :], apart[:, s, :], ALU.mult))
                order.wait()
                return nc.vector.scalar_tensor_tensor(var[:, s, :], apart[:, s, :], D / 4.0, both[:, s, :],
                                                      ALU.mult, ALU.add)

            def scale(s):
                order.mark(nc.vector.reciprocal(rstd[:, s, :], std[:, s, :]))
                order.wait()
                return nc.vector.scalar_tensor_tensor(nbias[:, s, :], mean2[:, s, :], -0.5, rstd[:, s, :],
                                                      ALU.mult, ALU.mult)

            def ln0_a(c):
                dve.wait_ge(x_loaded[c], 16)
                if c >= LN:
                    dve.wait_ge(ln0_h, c - LN + 1)
                stats(x_in[c], c % LN).then_inc(ln0_stats, 1)

            def ln0_b(c):
                dve.wait_ge(ln0_std, c + 1)
                scale(c % LN).then_inc(ln0_scale, 1)

            picks(0, 0, 1)
            ln0_a(0)
            picks(0, 1, 2)
            ln0_b(0)
            ln0_a(1)
            picks(0, 2, 3)
            ln0_b(1)
            picks(0, 3, 4)
            ln0_a(2)
            ln0_a(3)
            ln0_b(2)
            picks(0, 4, 5)
            ln0_b(3)
            ln0_a(4)
            picks(0, 5, 6)
            ln0_b(4)
            ln0_a(5)
            picks(0, 6, 7)
            ln0_b(5)
            picks(0, 7, 8)
            ln0_a(6)
            picks(0, 8, 9)
            ln0_b(6)
            ln0_a(7)
            picks(0, 9, 10)
            ln0_b(7)
            picks(0, 10, 20)

            def hid_low(b):
                dve.wait_ge(hid_hi, b + 1)
                nc.vector.scalar_tensor_tensor(hid[1], agg, 1.0 / PICK, hid[0], ALU.mult,
                                               ALU.subtract).then_inc(hid_lo, 1)

            def add_residual(b):
                dve.wait_ge(down_done, b + 1)
                dve.wait_ge(xres_ready, b + 1)
                nc.vector.tensor_tensor(x1, pa[:, 0:2, :].rearrange("p a (t d) -> p (a t) d", d=D), x1,
                                        ALU.add).then_inc(x1_ready, 1)
                dve.wait_ge(x1_ready, b + 1)
                stats(x1, LN).then_inc(ln1_stats, 1)

            def scale_h(b):
                dve.wait_ge(ln1_std, b + 1)
                scale(LN).then_inc(ln1_scale, 1)

            def h_low(b):
                dve.wait_ge(h2T_hi, b + 1)
                nc.vector.tensor_tensor(kT[1][:, :, bass.ts(b, BLK)], pa[:, 2:4, :],
                                        kT[0][:, :, bass.ts(b, BLK)], ALU.subtract).then_inc(h2T_lo, 1)

            def q_low(b):
                dve.wait_ge(q_hi, b + 1)
                nc.vector.tensor_tensor(q_out[:, 1], pa[:, 0:2, :], q_out[:, 0], ALU.subtract).then_inc(q_lo, 1)

            def v_low(b):
                dve.wait_ge(v_hi_s, b + 1)
                nc.vector.tensor_tensor(v_lo[:, bass.ts(b, E), :],
                                        pa[:, 0:2, :].rearrange("p a (t d) -> p (a t) d", d=D),
                                        v_hi[:, bass.ts(b, E), 0:D], ALU.subtract).then_inc(v_lo_s, 1)

            def iteration(b, end):
                picks(b + 1, 4, min(14, end))
                add_residual(b - 1)
                picks(b + 1, 14, min(15, end))
                scale_h(b - 1)
                picks(b + 1, 15, min(17, end))
                h_low(b - 1)
                picks(b + 1, 17, min(19, end))
                q_low(b - 1)
                picks(b + 1, 19, end)
                hid_low(b)
                v_low(b - 1)

            def weights_low():
                dve.wait_ge(qk_w_hi, 1)
                nc.vector.tensor_tensor(wqk[1], wqk_ps, wqk[0], ALU.subtract).then_inc(qk_w_lo, 1)

            picks(0, 20, 25)
            hid_low(0)
            weights_low()
            picks(0, 25, 35)
            add_residual(0)
            picks(0, 35, 36)
            scale_h(0)
            picks(0, 36, 39)
            h_low(0)
            picks(0, 39, 43)
            q_low(0)
            picks(0, 43, 47)
            v_low(0)
            picks(0, 47, 50)
            hid_low(1)
            picks(0, 50, 52)
            with dve.Fori(2, NB - 2) as b, order.loop(b, 2, NB - 2, 4 * 8 + 4):
                iteration(b, 20)
            iteration(NB - 2, 16)
            iteration(NB - 1, 4)

            def add_mask(i, g, jb, r):
                n = i * STEPS + g
                if r % 2 == 0:
                    m = i * NB + jb
                    dve.wait_ge(adj_in_loaded, 16 * (m + 1))
                    slot = adj_in[:, jb % NMASK]
                    nc.vector.tensor_scalar(slot, slot, 0x01010101, 0, ALU.bitwise_xor,
                                            ALU.logical_shift_left).then_inc(flipped, 1)
                    dve.wait_ge(flipped, m + 1)
                if not (i is 0 or i is 1 and isinstance(g, int) and g < 2):
                    dve.wait_ge(exp_done, n - RING + 1)
                for u in range(2):
                    dve.wait_ge(qk_done, 2 * n + u + 1)
                    bank = (2 * g + u) % 4 if i is 0 else u
                    nc.vector.scalar_tensor_tensor(
                        ring_tile[:, n % RING * 2 + u, :].rearrange("p (e i) -> p e i", e=E),
                        no_edge[:, jb % NMASK, 2 * (r % 2) + u], NEG,
                        sc[:, bank, :].rearrange("p (e i) -> p e i", e=E), ALU.mult, ALU.add).then_inc(copied, 1)

            def running_max(i, g):
                n = i * STEPS + g
                dve.wait_ge(copied, 2 * n + 2)
                if g is 1:
                    nc.vector.tensor_tensor(run_max, ring[:, (n + RING - 1) % RING], ring[:, n % RING],
                                            ALU.max).then_inc(maxed, 1)
                else:
                    dve.wait_ge(maxed, i * (STEPS - 1) + g - 1)
                    nc.vector.tensor_tensor(run_max, run_max, ring[:, n % RING], ALU.max).then_inc(maxed, 1)

            def column_max(i):
                dve.wait_ge(maxed, (i + 1) * (STEPS - 1))
                nc.vector.tensor_tensor(col_max, run_max[:, 0], run_max[:, 1], ALU.max).then_inc(colmax_ready, 1)

            def diagonal_max(i):
                dve.wait_ge(maxT_done, i + 1)
                order.mark(nc.vector.tensor_reduce(max_col, mc.rearrange("p (e q) -> p e q", e=E), axis=AX.X,
                                                   op=ALU.max))
                order.wait()
                order.mark(nc.vector.tensor_scalar(max_col, max_col, FLOOR, None, ALU.max))
                order.wait()
                nc.vector.tensor_tensor(diag_max, ident[:].unsqueeze(1).to_broadcast([P, E, P]),
                                        max_col.unsqueeze(2).to_broadcast([P, E, P]),
                                        ALU.mult).then_inc(diag_ready, 1)

            def shift(i, g):
                place = ring[:, (i * STEPS + g + RING - STEPS) % RING]
                nc.vector.tensor_tensor(place, place, mc.unsqueeze(1).to_broadcast([P, 2, BLK]),
                                        ALU.subtract).then_inc(shifted, 1)

            def finish(i):
                dve.wait_ge(pv_done, (i + 1) * STEPS)
                order.mark(nc.vector.tensor_scalar(den, acc[:, :, D], 1e-30, None, ALU.max))
                order.wait()
                order.mark(nc.vector.reciprocal(rden, den))
                dve.wait_ge(x1_loaded, 16 * (i + 1))
                order.wait()
                for e in range(E):
                    last = nc.vector.scalar_tensor_tensor(out_sb[:, e, :], acc[:, e, 0:D], rden[:, e:e + 1],
                                                          x1_in[:, e, :], ALU.mult, ALU.add)
                last.then_inc(out_ready, 1)

            def step(i, g, jb, r, scores=True, probs=True, finishes=False):
                if finishes:
                    finish(i - 2)
                if g is 0:
                    if scores:
                        add_mask(i, g, jb, r)
                    if probs:
                        diagonal_max(i - 1)
                        if i is 1:
                            add_mask(i, 1, jb, 1)
                        dve.wait_ge(max_spread, i)
                        shift(i, g)
                    return
                if probs:
                    shift(i, g)
                if scores:
                    if not (i is 1 and g is 1):
                        add_mask(i, g, jb, r)
                    running_max(i, g)

            def query_block(i, scores, probs, finishes):
                for r in range(4):
                    step(i, r, r // 2, r, scores, probs, finishes and r == 3)
                with dve.Fori(1, 4) as k:
                    for r in range(4):
                        step(i, 4 * k + r, 2 * k + r // 2, r, scores, probs)
                if scores:
                    column_max(i)

            for g in range(STEPS):
                step(0, g, g // 2, g % 4, probs=False)
                if g == 2:
                    add_residual(NB - 1)
                if g == 3:
                    scale_h(NB - 1)
                if g == 5:
                    h_low(NB - 1)
                if g == 7:
                    q_low(NB - 1)
                if g == 8:
                    v_low(NB - 1)
            dve.wait_ge(x1_stored, 16 * NB)
            dve.wait_ge(q_stored, 16 * NB)
            column_max(0)
            query_block(1, True, True, False)
            with dve.Fori(2, NB) as i, order.loop(i, 2, NB, 4):
                query_block(i, True, True, True)
            query_block(NB, False, True, True)
            finish(NB - 1)

        @block.scalar
        def _(act):
            act.wait_ge(dve_consts, 1)

            def ln0(c):
                act.wait_ge(ln0_stats, c + 1)
                nc.scalar.activation(std[:, c % LN, :], var[:, c % LN, :], ACT.Sqrt, scale=1.0 / D,
                                     bias=eps_col[:]).then_inc(ln0_std, 1)
                act.wait_ge(ln0_scale, c + 1)
                if c >= LN:
                    act.wait_ge(h_ready, c - LN + 1)
                for e in range(E):
                    last = nc.scalar.activation(h_f[c % LN][:, e, :], x_in[c][:, e, :], ACT.Relu,
                                                scale=rstd[:, c % LN, e:e + 1], bias=nbias[:, c % LN, e:e + 1])
                last.then_inc(ln0_h, 1)
                act.wait_ge(ln0_h, c + 1)
                nc.scalar.copy(h_hi[:, c * E:(c + 1) * E, :], h_f[c % LN]).then_inc(h_hi_ready, 1)

            def store_picks(b, q, h):
                act.wait_ge(tp_ready, 8 * b + 2 * q + h + 1)
                nc.scalar.copy(picked16[:, b % 2, 4 * h:4 * h + 4, 2 * P * q:2 * P * (q + 1)],
                               tp16[:, h, :].rearrange("p (c i) -> p c i", c=4)).then_inc(picks_stored, 1)

            def hid_high(b):
                act.wait_ge(agg_done, b + 1)
                nc.scalar.activation(hid[0], agg, ACT.Copy, scale=1.0 / PICK).then_inc(hid_hi, 1)

            def relu(b, c):
                act.wait_ge(up_done, HC * b + c + 1)
                if c >= 2:
                    act.wait_ge(act_lo, HC * b + c - 1)
                nc.scalar.activation(act_f[:, c % 2, :], pa[:, c, :], ACT.Relu, bias=b1_col[:, c:c + 1])
                nc.scalar.activation(act_h[0][:, c, :], pa[:, c, :], ACT.Relu,
                                     bias=b1_col[:, c:c + 1]).then_inc(act_ready, 1)

            def post_stage(b, s):
                if s == 0 or s == 1:
                    relu(b, 2 * s)
                    relu(b, 2 * s + 1)
                if s == 4:
                    act.wait_ge(ln1_stats, b + 1)
                    nc.scalar.activation(std[:, LN, :], var[:, LN, :], ACT.Sqrt, scale=1.0 / D,
                                         bias=eps_col[:]).then_inc(ln1_std, 1)
                if s == 5:
                    act.wait_ge(ln1_scale, b + 1)
                    for e in range(E):
                        last = nc.scalar.activation(h2[:, e, :], x1[:, e, :], ACT.Relu,
                                                    scale=rstd[:, LN, e:e + 1], bias=nbias[:, LN, e:e + 1])
                    last.then_inc(h2_ready, 1)
                if s == 6:
                    act.wait_ge(h2T_done, b + 1)
                    nc.scalar.copy(kT[0][:, :, bass.ts(b, BLK)], pa[:, 2:4, :]).then_inc(h2T_hi, 1)
                if s == 7:
                    act.wait_ge(q_done, b + 1)
                    nc.scalar.copy(q_out[:, 0], pa[:, 0:2, :]).then_inc(q_hi, 1)
                if s == 8:
                    act.wait_ge(v_done, b + 1)
                    nc.scalar.copy(v_hi[:, bass.ts(b, E), 0:D],
                                   pa[:, 0:2, :].rearrange("p a (t d) -> p (a t) d", d=D)).then_inc(v_hi_s, 1)

            def load_rows(b, q):
                act.dma_start(rows[:, q, :], adj_v[b, :, q, :]).then_inc(adj_loaded[q], 16)

            def load_mask(i, jb):
                if isinstance(jb, int) and jb >= NB:
                    i, jb = i + 1, jb - NB
                n = i * NB + jb
                early = i is 0 and isinstance(jb, int)
                if not (early and jb == 0):
                    act.wait_ge(adj_in_loaded, 16 * n)
                if not (early and jb < NMASK):
                    act.wait_ge(copied, E * (n - NMASK + 1))
                act.dma_start(adj_in[:, jb % NMASK].bitcast(U8),
                              adj_v[jb, :, :, bass.ts(i, BLK)]).then_inc(adj_in_loaded, 16)

            def store_tile(b, q, load=True):
                store_picks(b, q, 0)
                store_picks(b, q, 1)
                if load:
                    load_rows(b + 1, q)

            for c in range(NB):
                ln0(c)
                if c in (1, 5):
                    store_tile(0, c // 4)
            store_tile(0, 2)
            store_tile(0, 3)
            act.wait_ge(b_loaded, 32)

            def iteration(b, turn, load, late=False):
                for s in range(NB):
                    if late and s < NB - 1:
                        post_stage(b - 1, s)
                    if turn:
                        store_picks(b + 1, s // 2, s % 2)
                        if load and s % 2:
                            load_rows(b + 2, s // 2)
                    if not late or s == NB - 1:
                        post_stage(b - 1, s)
                hid_high(b)
                post_stage(b - 1, NB)

            hid_high(0)
            act.wait_ge(qk_w_done, 1)
            nc.scalar.copy(wqk[0], wqk_ps).then_inc(qk_w_hi, 1)
            store_tile(1, 0)
            store_tile(1, 1)
            post_stage(0, 0)
            post_stage(0, 1)
            store_tile(1, 2)
            post_stage(0, 4)
            post_stage(0, 5)
            store_tile(1, 3)
            post_stage(0, 6)
            post_stage(0, 7)
            store_tile(2, 0)
            post_stage(0, 8)
            store_tile(2, 1)
            hid_high(1)
            store_tile(2, 2)
            store_tile(2, 3)
            iteration(2, True, True, late=True)
            with act.Fori(3, NB - 2) as b:
                iteration(b, True, True)
            iteration(NB - 2, True, False)
            for jb in range(NMASK):
                load_mask(0, jb)
            iteration(NB - 1, False, False)
            for s, loads in ((0, ()), (1, ()), (4, (4,)), (5, (5,)), (6, ()), (7, (6, 7)), (8, (8, 9))):
                post_stage(NB - 1, s)
                for jb in loads:
                    load_mask(0, jb)

            def probs(i, g, slot):
                m = (i - 1) * STEPS + g
                act.wait_ge(shifted, m + 1)
                if not (i is 1 and isinstance(g, int) and g < NP):
                    act.wait_ge(pv_done, m - NP + 1)
                if not (i is 1 and isinstance(g, int) and g < 2):
                    act.wait_ge(p_ready, m - 1)
                place = ring[:, (m % RING)]
                nc.scalar.activation(p_hi[:, slot], place, ACT.Exp)
                nc.scalar.activation(p_f[:, slot % 2], place, ACT.Exp).then_inc(exp_done, 1)

            def query_block(i, loads=True, more=True):
                for r in range(4):
                    probs(i, r, r)
                    if loads and r % 2 == 0:
                        load_mask(i, 2 + r // 2)
                with act.Fori(1, 3) as k:
                    for r in range(4):
                        probs(i, 4 * k + r, r)
                        if loads and r % 2 == 0:
                            load_mask(i, 2 * k + 2 + r // 2)
                for r in range(4):
                    probs(i, 12 + r, r)
                    if loads and more and r % 2 == 0:
                        load_mask(i, NB + r // 2)

            query_block(1)
            with act.Fori(2, NB - 1) as i:
                query_block(i)
            query_block(NB - 1, more=False)
            query_block(NB, loads=False)

        @block.tensor
        def _(pe):
            rows_w = rows.bitcast(F32)
            terms = ((0, 0), (0, 1), (1, 0))

            def turn_picks(b, q, h, first=False, summed=None):
                pe.wait_ge(picks_ready, E * b + q + 1)
                if not first:
                    pe.wait_ge(picks_stored, 8 * b + 2 * q + h - 1)
                for c in range(4):
                    if summed is not None and c == 3:
                        await_sum(summed)
                    w = (4 * h + c) * P
                    last = nc.tensor.transpose(tp[:, h, c * P:(c + 1) * P], rows_w[:, q, w:w + P], ident[:])
                last.then_inc(tp_ready, 1)

            def await_sum(b):
                if b is not 0:
                    pe.wait_ge(hid_lo, b)
                pe.wait_ge(picks_stored, 8 * (b + 1))

            def sum_picks(b, c, par, first=0, n=E):
                cols = slice(first * P, (first + n) * P)
                if b is 0:
                    pe.wait_ge(h_ready, c + 1)
                for e in range(E):
                    for half in (h_hi, h_lo):
                        for d in range(DC):
                            nc.tensor.matmul(agg[:, d, cols], half[:, c * E + e, d * P:(d + 1) * P],
                                             picked8[:, par, c, cols, e],
                                             start=(c == 0 and e == 0 and half is h_hi and first == 0),
                                             stop=False, skip_group_check=n < E)
                if c == NB - 1 and first + n == E:
                    for e in range(E):
                        for half in (h_hi, h_lo):
                            for d in range(DC):
                                last = nc.tensor.matmul(agg[:, d, e * P:(e + 1) * P],
                                                        half[:, b * E + e, d * P:(d + 1) * P], ident16[:],
                                                        start=False, stop=(e == E - 1 and half is h_lo),
                                                        skip_group_check=n < E)
                    last.then_inc(agg_done, 1)

            def up(b, c):
                n = 0
                for s, t in terms:
                    for d in range(DC):
                        last = nc.tensor.matmul(pa[:, c, :], w1[s][:, d, c * P:(c + 1) * P], hid[t][:, d, :],
                                                start=(n == 0), stop=(n == 5))
                        n += 1
                last.then_inc(up_done, 1)

            def down(b):
                pe.wait_ge(act_lo, HC * (b + 1))
                for e in range(E):
                    n = 0
                    for s, t in terms:
                        for c in range(HC):
                            last = nc.tensor.matmul(pa[:, e // 2, (e % 2) * D:(e % 2 + 1) * D],
                                                    act_h[s][:, c, e * P:(e + 1) * P], w2[t][:, c, :],
                                                    start=(n == 0), stop=(n == 11))
                            n += 1
                last.then_inc(down_done, 1)

            def turn_h2(b):
                pe.wait_ge(h2_ready, b + 1)
                for d in range(DC):
                    for e in range(E):
                        last = nc.tensor.transpose(pa[:, 2 + d, e * P:(e + 1) * P], h2[:, e, d * P:(d + 1) * P],
                                                   ident[:])
                last.then_inc(h2T_done, 1)

            def project_q(b):
                pe.wait_ge(h2T_lo, b + 1)
                for d in range(DC):
                    n = 0
                    for s, t in terms:
                        for c in range(DC):
                            last = nc.tensor.matmul(pa[:, d, :], wqk[s][:, c, d * P:(d + 1) * P],
                                                    kT[t][:, c, bass.ts(b, BLK)], start=(n == 0), stop=(n == 5))
                            n += 1
                last.then_inc(q_done, 1)

            def project_v(b):
                pe.wait_ge(q_lo, b + 1)
                for e in range(E):
                    n = 0
                    for s, t in terms:
                        for c in range(DC):
                            last = nc.tensor.matmul(pa[:, e // 2, (e % 2) * D:(e % 2 + 1) * D],
                                                    kT[s][:, c, bass.ds(b * BLK + e * P, P)], wv[t][:, c, :],
                                                    start=(n == 0), stop=(n == 5))
                            n += 1
                last.then_inc(v_done, 1)

            def post_stage(b, s):
                if s == 0:
                    pe.wait_ge(hid_lo, b + 1)
                    pe.wait_ge(v_lo_s, b + 1)
                    up(b, 0)
                    up(b, 1)
                if s == 1:
                    up(b, 2)
                    up(b, 3)
                if s == 3:
                    down(b)
                if s == 5:
                    turn_h2(b)
                if s == 6:
                    project_q(b)
                if s == 7:
                    project_v(b)

            def weight_product():
                for a in range(DC):
                    n = 0
                    for s, t in terms:
                        for c in range(DC):
                            last = nc.tensor.matmul(wqk_ps[:, a, :], wq[s][:, c, a * P:(a + 1) * P], wk[t][:, c, :],
                                                    start=(n == 0), stop=(n == 5))
                            n += 1
                last.then_inc(qk_w_done, 1)

            def iteration(b, par, turn, late=False):
                for s in range(NB):
                    if turn and (not late or s == NB - 1):
                        turn_picks(b + 1, s // 2, s % 2, summed=b if s == 0 else None)
                    if s == 0 and (late or not turn):
                        await_sum(b)
                    sum_picks(b, s, par)
                    post_stage(b - 1, s)
                    if late and s < NB - 1:
                        turn_picks(b + 1, s // 2, s % 2)

            def keep_clock(n):
                for _ in range(n):
                    nc.tensor.matmul(pa[:, 3, 0:P], ones[:], ident[:], start=True, stop=True)

            def turn_tile(b, q, first=False):
                turn_picks(b, q, 0, first)
                turn_picks(b, q, 1, first)

            def sum_part(b, first, n, cs):
                pe.wait_ge(picks_stored, 8 * b + 2 * (first + n))
                for c in cs:
                    sum_picks(b, c, b % 2, first, n)

            pe.wait_ge(consts_ready, 4)
            with pe.Fori(0, 12):
                keep_clock(4)
            turn_tile(0, 0, first=True)
            sum_part(0, 0, 1, range(0, 5))
            turn_tile(0, 1)
            sum_part(0, 0, 1, (5,))
            sum_part(0, 1, 1, range(0, 6))
            turn_tile(0, 2)
            sum_part(0, 0, 1, (6,))
            sum_part(0, 1, 1, (6,))
            sum_part(0, 2, 1, range(0, 7))
            turn_tile(0, 3)
            for q in range(E - 1):
                sum_part(0, q, 1, (7,))
            sum_part(0, 3, 1, range(NB))
            pe.wait_ge(w_split, 5)
            weight_product()
            turn_tile(1, 0)
            turn_tile(1, 1)
            pe.wait_ge(qk_w_lo, 1)
            post_stage(0, 0)
            post_stage(0, 1)
            sum_part(1, 0, 2, range(0, 3))
            post_stage(0, 3)
            turn_tile(1, 2)
            sum_part(1, 0, 2, range(3, NB))
            turn_tile(1, 3)
            post_stage(0, 5)
            sum_part(1, 2, 2, range(0, 2))
            post_stage(0, 6)
            sum_part(1, 2, 2, range(2, 4))
            turn_tile(2, 0)
            post_stage(0, 7)
            turn_tile(2, 1)
            sum_part(1, 2, 2, range(4, NB))
            turn_tile(2, 2)
            turn_tile(2, 3)
            iteration(2, 0, True, late=True)
            with pe.Fori(1, NB // 2 - 1) as j:
                iteration(2 * j + 1, 1, True)
                iteration(2 * j + 2, 0, True)
            iteration(NB - 1, 1, False)

            def scores(i, g):
                for u in range(2):
                    tile = 2 * g + u
                    bank = tile % 4 if i is 0 else u
                    if i is 1 and g is 0:
                        pe.wait_ge(copied, 2 * STEPS - 3 + u)
                    elif i is not 0:
                        pe.wait_ge(copied, i * STEPS * 2 + tile - 1)
                    elif tile >= 4:
                        pe.wait_ge(copied, tile - 3)
                    n = 0
                    for s, w in terms:
                        for d in range(DC):
                            last = nc.tensor.matmul(sc[:, bank, :], kT[s][:, d, bass.ts(tile, P)], q_in[:, i % 2, w, d, :],
                                                    start=(n == 0), stop=(n == 5))
                            n += 1
                    last.then_inc(qk_done, 1)

            def attend(m, g, slot):
                pe.wait_ge(p_ready, m + 1)
                for u in range(2):
                    tile = 2 * g + u
                    first = g is 0 and u == 0
                    final = g is STEPS - 1 and u == 1
                    for e in range(E):
                        hi = p_hi[:, slot, u, e * P:(e + 1) * P]
                        lo = p_lo[:, slot, u, e * P:(e + 1) * P]
                        nc.tensor.matmul(acc[:, e, 0:D + 1], hi, v_hi[:, tile, 0:D + 1], start=first, stop=False)
                        nc.tensor.matmul(acc[:, e, 0:D], hi, v_lo[:, tile, :], start=False, stop=False)
                        last = nc.tensor.matmul(acc[:, e, 0:D + 1], lo, v_hi[:, tile, 0:D + 1], start=False,
                                                stop=final)
                last.then_inc(pv_done, 1)

            def turn_max(i):
                pe.wait_ge(colmax_ready, i + 1)
                for e in range(E):
                    last = nc.tensor.transpose(mc[:, e * P:(e + 1) * P], col_max[:, e * P:(e + 1) * P], ident[:])
                last.then_inc(maxT_done, 1)

            def spread_max(i):
                pe.wait_ge(diag_ready, i + 1)
                nc.tensor.matmul(mc, ones[:], diag_max.rearrange("p e q -> p (e q)"), start=True,
                                 stop=True).then_inc(max_spread, 1)

            def query_block(i, score, last_acc):
                base = i * STEPS - LAG
                if score:
                    pe.wait_ge(q_loaded, 16 * (i + 1))
                    scores(i, 0)
                turn_max(i - 1)
                if last_acc:
                    attend(base, 13, 1)
                if not last_acc:
                    scores(i, 1)
                spread_max(i - 1)
                for r in (1, 2):
                    if score and (last_acc or r == 2):
                        scores(i, r)
                    if last_acc:
                        attend(base + r, 13 + r, 1 + r)
                if score:
                    scores(i, 3)
                if last_acc:
                    pe.wait_ge(out_ready, i - 1)
                else:
                    pe.wait_ge(v_lo_s, NB + 1)
                attend(base + 3, 0, 0)
                with pe.Fori(1, 4) as k:
                    for r in range(4):
                        if score:
                            scores(i, 4 * k + r)
                        attend(base + 4 * k + r, 4 * k + r - 3, (r + 1) % NP)

            keep_clock(10)
            pe.wait_ge(q_loaded, 16)
            stages = {0: 0, 1: 1, 3: 3, 6: 5, 8: 6, 9: 7}
            for g in range(STEPS):
                if g in stages:
                    post_stage(NB - 1, stages[g])
                scores(0, g)
            query_block(1, True, False)
            with pe.Fori(2, NB) as i:
                query_block(i, True, True)
            query_block(NB, False, True)
            base = (NB + 1) * STEPS - LAG
            for r in range(3):
                attend(base + r, 13 + r, 1 + r)


_INS = ["x", "adj", "W1", "b1", "W2", "b2", "Wq", "Wk", "WvT"]


def kernel(x, adj, L0_gnn_W1, L0_gnn_b1, L0_gnn_W2, L0_gnn_b2, L1_gnn_Wq, L1_gnn_Wk, L1_gnn_Wv):
    import numpy as np
    import concourse.bacc as bacc
    from concourse.bass_utils import run_bass_kernel_spmd

    arrays = dict(zip(_INS, (
        np.ascontiguousarray(x), np.ascontiguousarray(adj),
        np.ascontiguousarray(L0_gnn_W1), np.ascontiguousarray(L0_gnn_b1),
        np.ascontiguousarray(L0_gnn_W2), np.ascontiguousarray(L0_gnn_b2),
        np.ascontiguousarray(L1_gnn_Wq), np.ascontiguousarray(L1_gnn_Wk),
        np.ascontiguousarray(np.asarray(L1_gnn_Wv).T))))
    nc = bacc.Bacc("TRN2", target_bir_lowering=False, num_devices=1)
    args = [nc.dram_tensor(f"in_{n}", a.shape, mybir.dt.from_np(a.dtype), kind="ExternalInput").ap()
            for n, a in arrays.items()]
    out = nc.dram_tensor("out", (N, D), F32, kind="ExternalOutput").ap()
    two_layers(nc, *args, out)
    r = run_bass_kernel_spmd(nc, [{f"in_{n}": a for n, a in arrays.items()}], core_ids=[0])
    return r.results[0]["out"]
```
